# Optimizing a Trainium2 kernel written in Bass

```python
import numpy as np
import jax
import jax.numpy as jnp

def _softmax(x, axis=-1):
    return jax.nn.softmax(x, axis=axis)

def _gelu(x):
    return jax.nn.gelu(x, approximate=True)

def _silu(x):
    return jax.nn.silu(x)

def _sigmoid(x):
    return jax.nn.sigmoid(x)

def _layernorm(x, axis=-1, eps=1e-05):
    m = jnp.mean(x, axis=axis, keepdims=True)
    v = jnp.var(x, axis=axis, keepdims=True)
    return (x - m) / jnp.sqrt(v + eps)

def _scatter_add(tgt, idx, src, axis=0):
    return tgt.at[idx].add(src)

def _segment_sum(src, seg, n):
    return jax.ops.segment_sum(src, seg, n)
kernel_name = 'mk_flamingo_gated_d1_seqx_r4_6d0349'

def setup_inputs(seed: int=0):
    np.random.seed(seed)
    _w = jnp.asarray

    def _rec_inputs():
        import jax
        import jax.numpy as jnp
        _rk = jax.random.key(seed)
        x = 7.22e-05 + 1 * jax.random.normal(jax.random.fold_in(_rk, 1), (4, 512, 256), jnp.float32)
        _lenS = 512 - jax.random.randint(jax.random.fold_in(_rk, 7), (4,), 0, max(1, 512 // 4) + 1, jnp.int32)
        _lenS2 = 1024 - jax.random.randint(jax.random.fold_in(_rk, 8), (4,), 0, max(1, 1024 // 4) + 1, jnp.int32)
        _ctx_1024P = jax.random.normal(jax.random.fold_in(_rk, 11), (4, 16, 256), jnp.float32)
        _ctx_1024c = jax.random.dirichlet(jax.random.fold_in(_rk, 511), 0.3 * jnp.ones((16,), jnp.float32), (4, 1024))
        _ctx_1024t = jnp.einsum('bsk,bkd->bsd', _ctx_1024c, _ctx_1024P)
        _ctx_1024t = _ctx_1024t * jax.lax.rsqrt(jnp.mean(jnp.square(_ctx_1024t)) + 1e-12) * 0.953939
        ctx_1024 = 4.13588e-05 + 0.999923 * (_ctx_1024t + 0.3 * jax.random.normal(jax.random.fold_in(_rk, 611), (4, 1024, 256), jnp.float32))
        _g = jax.random.normal(jax.random.fold_in(_rk, 9001), (2, 1), jnp.float32)
        _g = jnp.sign(_g) * jnp.maximum(jnp.abs(_g), 1.0) + (_g == 0) * 1.0
        g_xattn = _g[0]
        g_ffn = _g[1]
        return (x, ctx_1024, g_xattn, g_ffn)
    x, ctx_1024, g_xattn, g_ffn = _rec_inputs()

    def _L0_xattn_setup():
        import jax, jax.numpy as jnp
        import numpy as np
        D_MODEL = 256
        N_HEAD = 16

        def _split_heads(x, n_head):
            B, S, D = x.shape
            return x.reshape(B, S, n_head, D // n_head).transpose(0, 2, 1, 3)
        key = jax.random.key(seed)
        ks = jax.random.split(key, 12)
        B, S, D = (4, 512, D_MODEL)
        scale = 1.0 / np.sqrt(D)
        inp = {'Q': jax.random.normal(ks[0], (B, S, D), jnp.float32), 'K': jax.random.normal(ks[1], (B, S, D), jnp.float32), 'V': jax.random.normal(ks[2], (B, S, D), jnp.float32), 'Wq': jax.random.normal(ks[3], (D, D), jnp.float32) * scale, 'bq': jax.random.normal(ks[4], (D,), jnp.float32) * scale, 'Wk': jax.random.normal(ks[5], (D, D), jnp.float32) * scale, 'bk': jax.random.normal(ks[6], (D,), jnp.float32) * scale, 'Wv': jax.random.normal(ks[7], (D, D), jnp.float32) * scale, 'bv': jax.random.normal(ks[8], (D,), jnp.float32) * scale, 'Wo': jax.random.normal(ks[9], (D, D), jnp.float32) * scale, 'bo': jax.random.normal(ks[10], (D,), jnp.float32) * scale}
        return inp
    _L0_xattn_all = _L0_xattn_setup()
    _L0_xattn_in = {k: v for k, v in _L0_xattn_all.items() if k in ('Wq', 'bq', 'Wk', 'bk', 'Wv', 'bv', 'Wo', 'bo')}
    del _L0_xattn_all

    def _L0_ffn_setup():
        import jax, jax.numpy as jnp
        import numpy as np
        D_MODEL = 256
        FFN = 256
        N_EXPERTS = 8
        N_SHARED = 1
        TOP_K = 2
        B, S = (2, 512)

        def _swiglu(h):
            a, b = jnp.split(h, 2, axis=-1)
            return jax.nn.silu(a) * b
        key = jax.random.key(seed)
        ks = jax.random.split(key, 12)
        sc = 0.02
        return {'x': jax.random.normal(ks[0], (B, S, D_MODEL), dtype=jnp.float32), 'gate_w': jax.random.normal(ks[1], (D_MODEL, N_EXPERTS), dtype=jnp.float32) * sc, 'gate_b': jnp.zeros((N_EXPERTS,), dtype=jnp.float32), 'sw1': jax.random.normal(ks[2], (N_SHARED, D_MODEL, 2 * FFN), dtype=jnp.float32) * sc, 'sb1': jnp.zeros((N_SHARED, 2 * FFN), dtype=jnp.float32), 'sw2': jax.random.normal(ks[3], (N_SHARED, FFN, D_MODEL), dtype=jnp.float32) * sc, 'sb2': jnp.zeros((N_SHARED, D_MODEL), dtype=jnp.float32), 'rw1': jax.random.normal(ks[4], (N_EXPERTS, D_MODEL, 2 * FFN), dtype=jnp.float32) * sc, 'rb1': jnp.zeros((N_EXPERTS, 2 * FFN), dtype=jnp.float32), 'rw2': jax.random.normal(ks[5], (N_EXPERTS, FFN, D_MODEL), dtype=jnp.float32) * sc, 'rb2': jnp.zeros((N_EXPERTS, D_MODEL), dtype=jnp.float32)}
    _L0_ffn_all = _L0_ffn_setup()
    _L0_ffn_in = {k: v for k, v in _L0_ffn_all.items() if k in ('gate_w', 'gate_b', 'sw1', 'sb1', 'sw2', 'sb2', 'rw1', 'rb1', 'rw2', 'rb2')}
    del _L0_ffn_all
    return {'x': x, 'ctx_1024': ctx_1024, 'g_xattn': g_xattn, 'g_ffn': g_ffn, 'L0_xattn_Wq': _L0_xattn_in['Wq'], 'L0_xattn_bq': _L0_xattn_in['bq'], 'L0_xattn_Wk': _L0_xattn_in['Wk'], 'L0_xattn_bk': _L0_xattn_in['bk'], 'L0_xattn_Wv': _L0_xattn_in['Wv'], 'L0_xattn_bv': _L0_xattn_in['bv'], 'L0_xattn_Wo': _L0_xattn_in['Wo'], 'L0_xattn_bo': _L0_xattn_in['bo'], 'L0_ffn_gate_w': _L0_ffn_in['gate_w'], 'L0_ffn_gate_b': _L0_ffn_in['gate_b'], 'L0_ffn_sw1': _L0_ffn_in['sw1'], 'L0_ffn_sb1': _L0_ffn_in['sb1'], 'L0_ffn_sw2': _L0_ffn_in['sw2'], 'L0_ffn_sb2': _L0_ffn_in['sb2'], 'L0_ffn_rw1': _L0_ffn_in['rw1'], 'L0_ffn_rb1': _L0_ffn_in['rb1'], 'L0_ffn_rw2': _L0_ffn_in['rw2'], 'L0_ffn_rb2': _L0_ffn_in['rb2']}

def reference(x, ctx_1024, g_xattn, g_ffn, L0_xattn_Wq, L0_xattn_bq, L0_xattn_Wk, L0_xattn_bk, L0_xattn_Wv, L0_xattn_bv, L0_xattn_Wo, L0_xattn_bo, L0_ffn_gate_w, L0_ffn_gate_b, L0_ffn_sw1, L0_ffn_sb1, L0_ffn_sw2, L0_ffn_sb2, L0_ffn_rw1, L0_ffn_rb1, L0_ffn_rw2, L0_ffn_rb2):
    import jax
    import jax.numpy as jnp

    def _L0_xattn_ref(Q, K, V, Wq, bq, Wk, bk, Wv, bv, Wo, bo):
        import jax, jax.numpy as jnp
        import numpy as np
        D_MODEL = 256
        N_HEAD = 16

        def _split_heads(x, n_head):
            B, S, D = x.shape
            return x.reshape(B, S, n_head, D // n_head).transpose(0, 2, 1, 3)
        q = _split_heads(Q @ Wq.T + bq, N_HEAD)
        k = _split_heads(K @ Wk.T + bk, N_HEAD)
        v = _split_heads(V @ Wv.T + bv, N_HEAD)
        d_k = k.shape[-1]
        score = jnp.einsum('bhqd,bhkd->bhqk', q, k) / jnp.sqrt(jnp.float32(d_k))
        attn = jax.nn.softmax(score, axis=-1)
        out = jnp.einsum('bhqk,bhkd->bhqd', attn, v)
        B, H, S, dh = out.shape
        out = out.transpose(0, 2, 1, 3).reshape(B, S, H * dh)
        return out @ Wo.T + bo

    def _L0_ffn_ref(x, gate_w, gate_b, sw1, sb1, sw2, sb2, rw1, rb1, rw2, rb2):
        import jax, jax.numpy as jnp
        import numpy as np
        D_MODEL = 256
        FFN = 256
        N_EXPERTS = 8
        N_SHARED = 1
        TOP_K = 2
        B, S = (2, 512)

        def _swiglu(h):
            a, b = jnp.split(h, 2, axis=-1)
            return jax.nn.silu(a) * b
        hs = jnp.einsum('bsd,ndf->nbsf', x, sw1) + sb1[:, None, None, :]
        shared_out = jnp.einsum('nbsf,nfd->bsd', _swiglu(hs), sw2) + sb2.sum(0)
        probs = jax.nn.softmax(x @ gate_w + gate_b, axis=-1)
        topk_probs, topk_idx = jax.lax.top_k(probs, TOP_K)
        cw = jnp.sum(jax.nn.one_hot(topk_idx, N_EXPERTS, dtype=x.dtype) * topk_probs[..., None], axis=2)
        hr = jnp.einsum('bsd,edf->ebsf', x, rw1) + rb1[:, None, None, :]
        out_e = jnp.einsum('ebsf,efd->ebsd', _swiglu(hr), rw2) + rb2[:, None, None, :]
        routed_out = jnp.einsum('ebsd,bse->bsd', out_e, cw)
        return shared_out + routed_out
    x = x + jnp.tanh(g_xattn[0]) * _L0_xattn_ref(_layernorm(x, axis=-1), ctx_1024, ctx_1024, L0_xattn_Wq, L0_xattn_bq, L0_xattn_Wk, L0_xattn_bk, L0_xattn_Wv, L0_xattn_bv, L0_xattn_Wo, L0_xattn_bo)
    x = x + jnp.tanh(g_ffn[0]) * _L0_ffn_ref(_layernorm(x, axis=-1), L0_ffn_gate_w, L0_ffn_gate_b, L0_ffn_sw1, L0_ffn_sb1, L0_ffn_sw2, L0_ffn_sb2, L0_ffn_rw1, L0_ffn_rb1, L0_ffn_rw2, L0_ffn_rb2)
    return x

_drawn_inputs = setup_inputs


def setup_inputs(seed=0):
    import zlib

    import numpy as np

    out = dict(_drawn_inputs(seed))
    spreads = {'L0_ffn_gate_b': (0.0, 0.636),
     'L0_ffn_sb1': (0.0, 0.8),
     'L0_ffn_sb2': (0.0, 0.47),
     'L0_ffn_rb1': (0.0, 0.8),
     'L0_ffn_rb2': (0.0, 1.024)}
    factors = {'L0_xattn_bq': 5.717,
     'L0_xattn_bk': 64.0,
     'L0_ffn_gate_w': 3.01,
     'L0_ffn_sw1': 3.552,
     'L0_ffn_sw2': 3.54,
     'L0_ffn_rw1': 8.0,
     'L0_ffn_rw2': 8.0}
    for name, (base, spread) in spreads.items():
        noise = np.random.default_rng([zlib.crc32(name.encode()), seed]).standard_normal(out[name].shape)
        drawn = base * np.exp(spread * noise) if base else spread * noise
        out[name] = jnp.asarray(drawn.astype(out[name].dtype))
    for name, factor in factors.items():
        out[name] = (out[name] * factor).astype(out[name].dtype)
    return out
```

```python
from contextlib import ExitStack

import concourse.bass as bass
from concourse import mybir

F32 = mybir.dt.float32
F32R = mybir.dt.float32r
BF16 = mybir.dt.bfloat16
ALU = mybir.AluOpType
ACT = mybir.ActivationFunctionType
X_AXIS = mybir.AxisListType.X

P = 128
NB, NQ, NK, D = 4, 512, 1024, 256
NH, DH = 16, 16
DT = D // P
QT = NQ // P
KT = NK // P
HG = 4
NG = NH // HG
UNITS = NB * NG
TERMS = ((0, 0), (0, 1), (1, 0), (1, 1), (0, 2), (2, 0))
SROWS = len(TERMS) * DH
MROWS = SROWS + 3
VW = 32
NE = 9
NR = NE - 1
FF = 256
EARLY = 6
WCOLS = DT * 2 * FF + DT * D
BLK = 512
EPS = 1e-5
SCALE = 1.0 / DH ** 0.5


def build(nc, x, ctx_in, gates, wqkv, bqkv, wo, bo, gate_w, gate_b, wexp, b1, b2, ident, tri, out):
    dram = lambda name, shape, dt: nc.dram_tensor(name, shape, dt, kind="Internal").ap()
    q_parts = dram("q_parts", [NB, 3, D, NQ], BF16)
    k_parts = dram("k_parts", [NB, 3, D, NK], BF16)
    v_pad = dram("v_pad", [NB, KT, P, NH * VW], F32)
    attn = dram("attn", [NB, P, QT, D], F32)
    cw_rows = dram("cw_rows", [NR, NB * NQ], F32)

    with ExitStack() as es:
        sb = lambda name, shape, dt=F32, st=es: st.enter_context(nc.sbuf_tensor(name, shape, dt))
        ps = lambda name, shape, st=es: st.enter_context(nc.psum_tensor(name, shape, F32))
        sem = lambda name: es.enter_context(nc.semaphore(name))

        xs = sb("xs", [P, NB * QT, D])
        idn = sb("idn", [P, P])
        eW1H = sb("eW1H", [P, EARLY, DT, 2 * FF], F32R)
        eW1L = sb("eW1L", [P, EARLY, DT, 2 * FF], F32R)
        eW2H = sb("eW2H", [P, EARLY, DT, D], F32R)
        eW2L = sb("eW2L", [P, EARLY, DT, D], F32R)
        wraw = sb("wraw", [P, 2, WCOLS])
        trimask = sb("trimask", [P, NR, NR])
        tg_in = sb("tg_in", [P, 2])
        tg = sb("tg", [P, 2])
        bq_s = sb("bq_s", [P, 3, DT])
        gb_s = sb("gb_s", [NR, 1])
        gw_raw = sb("gw_raw", [P, DT, NR])
        gwH = sb("gwH", [P, DT, NR], F32R)
        gwL = sb("gwL", [P, DT, NR], F32R)
        blank = sb("blank", [P, 1])
        stats = sb("stats", [P, QT, 6])
        mv = sb("mv", [P, QT, 2])
        veps = sb("veps", [P, QT])
        std = sb("std", [P, QT])
        rstd = sb("rstd", [P, QT])
        nt = sb("nt", [P, QT])

        sa = ExitStack()
        wA_raw = sb("wA_raw", [P, 3, DT, D], F32, sa)
        wAH = sb("wAH", [P, 3, DT, D], F32R, sa)
        wAL = sb("wAL", [P, 3, DT, D], F32R, sa)
        ctxt = sb("ctxt", [P, 2, QT, D], F32, sa)
        zA = sb("zA", [P, QT, D], F32, sa)
        tH = sb("tH", [P, 2, DT, BLK], F32R, sa)
        tL = sb("tL", [P, 2, DT, BLK], F32R, sa)
        kf = sb("kf", [P, 2, BLK], F32, sa)
        r1 = sb("r1", [P, 2, BLK], F32, sa)
        parts = sb("parts", [P, 3, DT, 3, BLK], BF16, sa)
        vst = sb("vst", [P, 4, 2, NH, VW], F32, sa)
        sa.close()
        sB = ExitStack()
        kst = sb("kst", [MROWS, NG, HG, NK], BF16, sB)
        qst = sb("qst", [MROWS, NG, HG, NQ], BF16, sB)
        vt = sb("vt", [P, NG, KT, HG * VW], F32, sB)
        pr = sb("pr", [P, 4, HG, NQ], F32, sB)
        osb = sb("osb", [P, NQ], F32, sB)
        mneg = sb("mneg", [P, 2, HG * QT], F32, sB)
        msb = sb("msb", [HG * QT, 2, 3, P], BF16, sB)
        mres = sb("mres", [HG * QT, P], F32, sB)
        rden = sb("rden", [P, QT, HG], F32, sB)
        ast = sb("ast", [P, 2, QT, HG * DH], F32, sB)
        sB.close()
        lW1H = sb("lW1H", [P, NE - EARLY, DT, 2 * FF], F32R)
        lW1L = sb("lW1L", [P, NE - EARLY, DT, 2 * FF], F32R)
        lW2H = sb("lW2H", [P, NE - EARLY, DT, D], F32R)
        lW2L = sb("lW2L", [P, NE - EARLY, DT, D], F32R)
        zTH = sb("zTH", [P, 2, DT, BLK], F32R)
        zTL = sb("zTL", [P, 2, DT, BLK], F32R)
        a_in = sb("a_in", [P, QT, D])
        aT = sb("aT", [P, DT, BLK])
        wo_s = sb("wo_s", [P, DT, D])
        bo_s = sb("bo_s", [P, D])
        z2 = sb("z2", [P, QT, D])
        lT = sb("lT", [NR, BLK])
        pt = sb("pt", [P, 4, QT, NR])
        small = sb("small", [P, 3, QT])
        cmp = sb("cmp", [P, 2, QT * NR, NR])
        rank = sb("rank", [P, QT * NR])
        cwT = sb("cwT", [NE, 2, BLK])
        cwb = sb("cwb", [P, 2, BLK])
        b1_s = sb("b1_s", [P, NE, 4])
        b2_s = sb("b2_s", [NE, D])
        sil = sb("sil", [P, 2, BLK])
        g = sb("g", [P, 2, BLK])
        gH = sb("gH", [P, 2, 2, BLK], F32R)
        gL = sb("gL", [P, 2, 2, BLK], F32R)
        yT = aT
        o_s = z2

        pa = ExitStack()
        psT = ps("psT", [P, 2, DT, BLK], pa)
        psF = ps("psF", [P, DT, BLK], pa)
        psV = ps("psV", [P, 2, 2, D], pa)
        pa.close()
        pb = ExitStack()
        psM = ps("psM", [P, 2, NK], pb)
        psS = ps("psS", [P, 2, NQ], pb)
        psO = ps("psO", [P, 2, NQ], pb)
        pb.close()
        psH = ps("psH", [P, 2, 2, BLK])
        psY = ps("psY", [P, 2, BLK])
        psX = ps("psX", [P, 2, BLK])

        consts = sem("consts")
        wA_in = sem("wA_in")
        x0_in = sem("x0_in"); x_in = sem("x_in")
        ctx_ld = [sem("ctx_in0"), sem("ctx_in1")]
        c_in = sem("c_in")
        wA_hi = sem("wA_hi"); wA_ok = sem("wA_ok")
        gw_ok = sem("gw_ok")
        dchain = sem("dve_chain")
        tanh_ok = sem("tanh_ok")
        var_ok = sem("var_ok"); std_ok = sem("std_ok"); z_ok = sem("z_ok")
        t_full = sem("t_full"); t_hi = sem("t_hi"); t_split = sem("t_split")
        f_full = sem("f_full"); f_taken = sem("f_taken"); r_ok = sem("r_ok"); k_ok = sem("k_parts_ok")
        v_full = sem("v_full"); v_taken = sem("v_taken")
        qk_st = [sem(f"parts_stored{c}") for c in range(3)]
        v_st = [sem(f"v_stored{s}") for s in range(4)]
        pads = sem("pads"); ones_k = sem("ones_k"); cw_ones = sem("cw_ones")
        unit_ld = [sem(f"unit_in{s}") for s in range(NG)]
        m_ld = [sem(f"max_in{s}") for s in range(NG)]
        m_full = sem("m_full"); m_free = sem("m_free")
        mt_full = sem("mt_full"); mt_split = sem("mt_split")
        s_full = sem("s_full"); e_done = sem("exp_done")
        pv_done = sem("pv_done")
        o_copied = sem("o_copied"); ot_full = sem("ot_full"); o_taken = sem("o_taken")
        a_st = [sem("a_stored0"), sem("a_stored1")]
        raw_ld = [sem("raw_in0"), sem("raw_in1")]
        pool_c = sem("pool_chain"); w_ok = sem("w_ok")
        a_ld = sem("a_in"); at_full = sem("at_full"); at_ok = sem("at_ok")
        wo_full = sem("wo_full"); z2_ok = sem("z2_ok"); zt_full = sem("zt_full")
        zt_hi = sem("zt_hi"); zt_ok = sem("zt_ok")
        lg_full = sem("lg_full"); lg_sb = sem("lg_sb"); lt_full = sem("lt_full")
        d_ok = sem("d_ok"); ex_ok = sem("ex_ok"); cw_ok = sem("cw_ok")
        cwt_full = sem("cwt_full"); cwt_ok = sem("cwt_ok"); cw_st = sem("cw_stored")
        cwb_ld = [sem("cwb_in0"), sem("cwb_in1")]
        h_full = sem("h_full"); sil_ok = sem("sil_ok"); g_ok = sem("g_ok")
        gh_ok = sem("gh_ok"); gl_ok = sem("gl_ok"); w2_done = sem("w2_done")
        y_copied = sem("y_copied"); yt_full = sem("yt_full")
        y_taken = sem("y_taken"); out_st = sem("out_stored")

        def w1(e, part):
            t = ((eW1H, eW1L), (lW1H, lW1L))[e >= EARLY][part]
            return t[:, e % EARLY]

        def w2(e, part):
            t = ((eW2H, eW2L), (lW2H, lW2L))[e >= EARLY][part]
            return t[:, e % EARLY]

        def cw_of(b):
            return cwT[:, bass.ds(b % 2, 1)].rearrange("e a t -> e (a t)")

        TILES = HG * QT
        FIRST = 10
        REST = TILES - FIRST
        AHEAD = TILES + FIRST
        LEAD = 2

        def max_tiles(u, step):
            for j in (2 * step, 2 * step + 1):
                yield (j, 1, FIRST + j) if j < REST else (j, 2, j - REST)

        def exists(last, u):
            return not last or u < NG

        block = es.enter_context(nc.Block())

        @block.sync
        def _(sp):
            sp.dma_start(xs[:, 0:QT, :], x[0].rearrange("(t p) d -> p t d", p=P)).then_inc(x0_in, 16)
            sp.dma_start(wA_raw[:], wqkv).then_inc(wA_in, 16)
            sp.dma_start(idn[:], ident).then_inc(consts, 16)
            sp.dma_start(tg_in[:], gates).then_inc(consts, 16)
            sp.dma_start(bq_s[:], bqkv).then_inc(consts, 16)
            sp.dma_start(gw_raw[:], gate_w).then_inc(consts, 16)
            sp.dma_start(gb_s[:], gate_b).then_inc(consts, 16)
            sp.dma_start(trimask[:], tri).then_inc(consts, 16)
            for h in range(2):
                sp.dma_start(ctxt[:, h], ctx_in[0, h * BLK:(h + 1) * BLK].rearrange("(t p) d -> p t d", p=P)
                             ).then_inc(ctx_ld[h], 16)
            for b in range(1, NB):
                sp.dma_start(xs[:, b * QT:(b + 1) * QT, :],
                             x[b].rearrange("(t p) d -> p t d", p=P)).then_inc(x_in, 16)

            def stores(b, load_next):
                for c in range(3):
                    if c < 2 and load_next:
                        sp.wait_ge(t_full, 6 * b + 2 * c + 4)
                        sp.dma_start(ctxt[:, c], ctx_in[b + 1, c * BLK:(c + 1) * BLK].rearrange(
                            "(t p) d -> p t d", p=P)).then_inc(ctx_ld[c], 16)
                    for m in range(DT):
                        sp.wait_ge(k_ok, 2 + 6 * b + 2 * c + m + 1)
                        dst = q_parts[b] if c == 0 else k_parts[b, :, :, (c - 1) * BLK:c * BLK]
                        sp.dma_start(dst[:, m * P:(m + 1) * P, :].rearrange("s p t -> p s t"),
                                     parts[:, c, m]).then_inc(qk_st[c], 16)
                    if c:
                        for s in range(2):
                            slot = 2 * (c - 1) + s
                            sp.wait_ge(v_taken, 2 + 4 * b + slot + 1)
                            sp.dma_start(v_pad[b, 2 * slot:2 * slot + 2].rearrange("t p c -> p t c"),
                                         vst[:, slot].rearrange("p t h v -> p t (h v)")).then_inc(v_st[slot], 16)

            with sp.Fori(0, NB - 1) as b:
                stores(b, True)
            stores(NB - 1, False)

            def load_unit(b, u):
                for t, (qp, kp) in enumerate(TERMS):
                    rows = slice(t * DH, (t + 1) * DH)
                    heads = slice(u * HG * DH, (u + 1) * HG * DH)
                    sp.dma_start(qst[rows, u], q_parts[b, qp, heads, :].rearrange("(h d) t -> d h t", d=DH)
                                 ).then_inc(unit_ld[u], 16)
                    sp.dma_start(kst[rows, u], k_parts[b, kp, heads, :].rearrange("(h d) t -> d h t", d=DH)
                                 ).then_inc(unit_ld[u], 16)
                sp.dma_start(vt[:, u], v_pad[b, :, :, u * HG * VW:(u + 1) * HG * VW].rearrange("k p c -> p k c")
                             ).then_inc(unit_ld[u], 16)

            def load_max(b, u):
                for s in range(3):
                    sp.dma_start(qst[SROWS + s:SROWS + s + 1, u], msb[:, u % 2, s, :]).then_inc(m_ld[u], 16)

            for c in range(3):
                sp.wait_ge(qk_st[c], 32 + 32 * NB)
            for s in range(4):
                sp.wait_ge(v_st[s], 16 + 16 * NB)
            sp.wait_ge(f_full, 4 + 6 * NB)
            for u in range(NG):
                load_unit(0, u)
            sp.wait_ge(mt_split, 1)
            load_max(0, 0)

            def unit_dmas(b, u, last):
                if exists(last, u + 1):
                    sp.wait_ge(mt_split, 4 * b + u + 2)
                    load_max(b, (u + 1) % NG)
                if not last:
                    sp.wait_ge(pv_done, 4 + KT * (4 * b + u + 1))
                    load_unit(b + 1, u)
                sp.wait_ge(o_taken, 4 * b + u + 2)
                sp.dma_start(attn[b, :, :, u * HG * DH:(u + 1) * HG * DH], ast[:, u % 2]).then_inc(a_st[u % 2], 16)

            with sp.Fori(0, NB - 1) as b:
                for u in range(NG):
                    unit_dmas(b, u, False)
            for u in range(NG):
                unit_dmas(NB - 1, u, True)
            for s in range(2):
                sp.wait_ge(a_st[s], 16 + 16 * UNITS // 2)
            sp.dma_start(a_in[:], attn[0]).then_inc(a_ld, 16)
            sp.dma_start(wo_s[:], wo).then_inc(c_in, 16)
            sp.dma_start(bo_s[:], bo).then_inc(c_in, 16)
            sp.dma_start(b1_s[:], b1).then_inc(c_in, 16)
            sp.dma_start(b2_s[:], b2).then_inc(c_in, 16)

            def store_weights(b):
                sp.wait_ge(cwt_ok, b + 1)
                cols = bass.ds(b * BLK, BLK)
                sp.dma_start(cw_rows[:, cols], cw_of(b)[0:NR]).then_inc(cw_st, 16)

            def expert_dmas(b, last):
                sp.wait_ge(cw_st, 16 * (b + 1))
                for e in range(1, NE):
                    sp.wait_ge(g_ok, 2 + 18 * b + (2 * (e - 1) if e > 2 else 0))
                    row = cw_rows[e - 1:e, bass.ds(b * BLK, BLK)]
                    sp.dma_start(cwb[:, e % 2, :], row.to_broadcast([P, BLK])).then_inc(cwb_ld[e % 2], 16)
                if not last:
                    sp.wait_ge(at_full, b + 2)
                    sp.dma_start(a_in[:], attn[(b + 2) % NB]).then_inc(a_ld, 16)
                    store_weights(b + 1)
                sp.wait_ge(y_taken, b + 2)
                sp.dma_start(out[b].rearrange("(t p) d -> p t d", p=P), o_s[:]).then_inc(out_st, 16)

            sp.wait_ge(at_full, 1)
            sp.dma_start(a_in[:], attn[1]).then_inc(a_ld, 16)
            store_weights(0)
            with sp.Fori(0, NB - 1) as b:
                expert_dmas(b, False)
            expert_dmas(NB - 1, True)
            sp.wait_ge(out_st, 16 + 16 * NB)
            sp.wait_ge(a_ld, 16 * (NB + 1))

        @block.gpsimd
        def _(pool):
            nc.gpsimd.dma_start(wraw[:, 0], wexp[0]).then_inc(raw_ld[0], 16)
            nc.gpsimd.dma_start(wraw[:, 1], wexp[1]).then_inc(raw_ld[1], 16)
            for s, n in ((f_full, 4), (f_taken, 2), (k_ok, 2), (v_taken, 2), (m_free, 2), (e_done, 2),
                         (pv_done, 4), (o_taken, 1), (g_ok, 2), (w2_done, 2), (y_taken, 1), (out_st, 16)):
                pool.sem_inc(s, n)
            for c in range(3):
                pool.sem_inc(qk_st[c], 32)
            for s in range(4):
                pool.sem_inc(v_st[s], 16)
            for s in range(2):
                pool.sem_inc(a_st[s], 16)
            nc.gpsimd.memset(vst[:, :, :, :, DH:VW].rearrange("p a b h v -> p (a b h) v"), 0.0).then_inc(pool_c, 1)
            pool.wait_ge(pool_c, 1)
            nc.gpsimd.memset(vst[:, :, :, :, DH:DH + 1].rearrange("p a b h v -> p (a b h) v"), 1.0).then_inc(pads, 1)

            def third_parts(b):
                for c in range(3):
                    for m in range(DT):
                        pool.wait_ge(r_ok, 6 * b + 2 * c + m + 1)
                        nc.gpsimd.tensor_tensor(parts[:, c, m, 2], r1[:, m], parts[:, c, m, 1],
                                                ALU.subtract).then_inc(k_ok, 1)

            with pool.Fori(0, NB) as b:
                third_parts(b)

            for c in range(3):
                pool.wait_ge(qk_st[c], 32 + 32 * NB)
            for s in range(4):
                pool.wait_ge(v_st[s], 16 + 16 * NB)
            pool.wait_ge(f_full, 4 + 6 * NB)
            nc.gpsimd.memset(kst[SROWS:MROWS], 1.0).then_inc(ones_k, 1)
            pool.wait_ge(ones_k, 1)

            def prepare(e, r, outs):
                nw1 = DT * 2 * FF
                base = 1 + 3 * e
                hi1, lo1, hi2, lo2 = outs
                raw1, raw2 = wraw[:, r, 0:nw1], wraw[:, r, nw1:WCOLS]
                nc.gpsimd.tensor_copy(hi1, raw1).then_inc(pool_c, 1)
                pool.wait_ge(pool_c, base + 1)
                nc.gpsimd.tensor_tensor(lo1, raw1, hi1.bitcast(F32), ALU.subtract).then_inc(pool_c, 1)
                nc.gpsimd.tensor_copy(hi2, raw2).then_inc(pool_c, 1)
                pool.wait_ge(pool_c, base + 3)
                nc.gpsimd.tensor_tensor(lo2, raw2, hi2.bitcast(F32), ALU.subtract).then_inc(w_ok, 1)
                pool.wait_ge(w_ok, e + 1)

            def flat(tensors, e):
                return tuple(t[:, bass.ds(e, 1)].rearrange("p a k c -> p (a k c)") for t in tensors)

            with pool.Fori(0, EARLY // 2) as i:
                for r in range(2):
                    e = i * 2 + r
                    pool.wait_ge(raw_ld[r], 16 * (i + 1))
                    prepare(e, r, flat((eW1H, eW1L, eW2H, eW2L), e))
                    nc.gpsimd.dma_start(wraw[:, r], wexp[e + 2]).then_inc(raw_ld[r], 16)
            pool.wait_ge(ot_full, UNITS)
            for s in range(2):
                pool.wait_ge(a_st[s], 16 + 16 * UNITS // 2)
            nc.gpsimd.memset(cwT[:], 1.0).then_inc(cw_ones, 1)
            pool.wait_ge(cw_ones, 1)
            for e in range(EARLY, NE):
                r = e % 2
                pool.wait_ge(raw_ld[r], 16 * (e // 2 + 1))
                prepare(e, r, flat((lW1H, lW1L, lW2H, lW2L), e - EARLY))
                if e + 2 < NE:
                    nc.gpsimd.dma_start(wraw[:, r], wexp[e + 2]).then_inc(raw_ld[r], 16)

        @block.scalar
        def _(act):
            def sqrt_of(n):
                act.wait_ge(var_ok, n)
                nc.scalar.activation(std[:], veps[:], ACT.Sqrt).then_inc(std_ok, 1)

            act.wait_ge(wA_in, 16)
            nc.scalar.copy(wAH[:].rearrange("p a k c -> p (a k c)"),
                           wA_raw[:].rearrange("p a k c -> p (a k c)")).then_inc(wA_hi, 1)
            act.wait_ge(consts, 16 * 6)
            sqrt_of(1)
            act.wait_ge(pads, 1)

            def phase_a(b):
                def high(c):
                    buf = c % 2
                    act.wait_ge(f_full, 6 * b + (4, 2, 6)[c])
                    for k in range(DT):
                        act.wait_ge(t_full, 6 * b + 2 * c + k + 1)
                        nc.scalar.copy(tH[:, buf, k], psT[:, buf, k]).then_inc(t_hi, 1)

                def biased(c):
                    for m in range(DT):
                        i = 6 * b + 2 * c + m
                        act.wait_ge(f_full, 4 + i + 1)
                        act.wait_ge(k_ok, i + 1)
                        act.wait_ge(qk_st[c], 32 * (b + 1))
                        bias = bq_s[:, min(c, 1), m:m + 1]
                        nc.scalar.activation(kf[:, m], psF[:, m], ACT.Identity, bias=bias)
                        nc.scalar.activation(parts[:, c, m, 0], psF[:, m], ACT.Identity,
                                             bias=bias).then_inc(f_taken, 1)

                def values(c):
                    for s in range(2):
                        slot = 2 * (c - 1) + s
                        act.wait_ge(v_full, 4 * b + slot + 1)
                        act.wait_ge(v_st[slot], 16 * (b + 1))
                        nc.scalar.copy(vst[:, slot, :, :, 0:DH], psV[:, s].rearrange("p t (h d) -> p t h d", d=DH)
                                       ).then_inc(v_taken, 1)

                high(0)
                high(1)
                biased(0)
                high(2)
                sqrt_of(b + 2)
                biased(1)
                values(1)
                biased(2)
                values(2)

            with act.Fori(0, NB) as b:
                phase_a(b)

            nc.scalar.activation(tg[:], tg_in[:], ACT.Tanh).then_inc(tanh_ok, 1)

            def exponentials(s, slot, j):
                if j == 0:
                    act.wait_ge(pv_done, s + 1)
                act.wait_ge(s_full, 4 * s + j + 1)
                nc.scalar.activation(pr[:, slot, j], psS[:, j % 2], ACT.Exp, scale=SCALE).then_inc(e_done, 1)

            for s in range(LEAD):
                for j in range(HG):
                    exponentials(s, s % 4, j)

            def unit_exps(b, u, last):
                n = 4 * b + u
                for k in range(KT):
                    ahead = exists(last, u + (k + LEAD) // KT)
                    for j in range(HG):
                        if ahead:
                            exponentials(8 * n + k + LEAD, (k + LEAD) % 4, j)
                        if k == KT - 1 and j == 1:
                            act.wait_ge(pv_done, 4 + KT * (n + 1))
                            nc.scalar.copy(osb[:], psO[:, u % 2]).then_inc(o_copied, 1)

            with act.Fori(0, NB - 1) as b:
                for u in range(NG):
                    unit_exps(b, u, False)
            for u in range(NG):
                unit_exps(NB - 1, u, True)

            def r_attn(b):
                act.wait_ge(at_full, b + 1)
                for k in range(DT):
                    nc.scalar.activation(aT[:, k], psX[:, k], ACT.Identity,
                                         bias=bq_s[:, 2, k:k + 1]).then_inc(at_ok, 1)

            def r_sqrt(b):
                sqrt_of(NB + 2 + b)

            def r_high(b):
                act.wait_ge(zt_full, b + 1)
                for k in range(DT):
                    nc.scalar.copy(zTH[:, bass.ds(b % 2, 1), k].rearrange("p a c -> p (a c)"), psX[:, k]).then_inc(zt_hi, 1)

            def r_logits(b):
                act.wait_ge(lg_full, b + 1)
                nc.scalar.activation(lT[:], psX[0:NR, 0], ACT.Identity, bias=gb_s[:, 0:1]).then_inc(lg_sb, 1)

            def r_exp(b):
                act.wait_ge(d_ok, b + 1)
                nc.scalar.activation(pt[:, 1], pt[:, 0], ACT.Exp).then_inc(ex_ok, 1)

            def r_cwt(b):
                act.wait_ge(cwt_full, b + 1)
                nc.scalar.copy(cw_of(b)[0:NR], psX[0:NR, 0]).then_inc(cwt_ok, 1)

            router = {0: r_attn, 2: r_sqrt, 3: r_high, 4: r_logits, 5: r_exp, 7: r_cwt}

            act.wait_ge(c_in, 16 * 4)
            act.wait_ge(cw_ones, 1)
            for f in router.values():
                f(0)

            def experts(b, last):
                for e in range(NE):
                    for j in range(2):
                        q = 18 * b + 2 * e + j
                        act.wait_ge(h_full, q + 1)
                        nc.scalar.activation(sil[:, j], psH[:, j, 0], ACT.Silu,
                                             bias=b1_s[:, e, j:j + 1]).then_inc(sil_ok, 1)
                        if j == 0:
                            act.wait_ge(w2_done, 9 * b + (e + 1 if e else 2))
                        act.wait_ge(g_ok, 2 + q + 1)
                        nc.scalar.copy(gH[:, e % 2, j], g[:, j]).then_inc(gh_ok, 1)
                    if not last and e in router:
                        router[e](b + 1)
                act.wait_ge(w2_done, 2 + 9 * (b + 1))
                for m in range(DT):
                    nc.scalar.copy(yT[:, m], psY[:, m]).then_inc(y_copied, 1)

            with act.Fori(0, NB - 1) as b:
                experts(b, False)
            experts(NB - 1, True)

        @block.vector
        def _(dve):
            V = nc.vector
            def chain(ins, value):
                ins.then_inc(dchain, 1)
                dve.wait_ge(dchain, value)

            NORM1, NORM2 = 3, 7

            def variances(rows, base):
                V.memset(blank[:], 0.0)
                for t in range(QT):
                    last = V.bn_stats(stats[:, t], rows(t))
                chain(last, base + 1)
                V.memset(blank[:], 0.0)
                for t in range(QT):
                    last = V.bn_aggr(mv[:, t], stats[:, t])
                chain(last, base + 2)
                V.tensor_scalar(veps[:], mv[:, :, 1], EPS, None, ALU.add).then_inc(var_ok, 1)

            def normalise(rows, dst, done, nth, base):
                dve.wait_ge(std_ok, nth)
                chain(V.reciprocal(rstd[:], std[:]), base + 1)
                chain(V.tensor_tensor(nt[:], rstd[:], rstd[:], ALU.mult), base + 2)
                chain(V.tensor_tensor(nt[:], nt[:], veps[:], ALU.mult), base + 3)
                chain(V.tensor_scalar(nt[:], nt[:], -0.5, 1.5, ALU.mult, ALU.add), base + 4)
                chain(V.tensor_tensor(rstd[:], rstd[:], nt[:], ALU.mult), base + 5)
                for t in range(QT):
                    last = V.tensor_scalar(dst[:, t], rows(t), mv[:, t, 0:1], rstd[:, t:t + 1],
                                           ALU.subtract, ALU.mult)
                last.then_inc(done, 1)

            def x_rows(b):
                return lambda t: xs[:, bass.ds(b * QT + t, 1)].rearrange("p a d -> p (a d)")

            dve.wait_ge(x0_in, 16)
            variances(x_rows(0), 0)
            dve.wait_ge(wA_hi, 1)
            V.tensor_tensor(wAL[:].rearrange("p a k c -> p (a k c)"), wA_raw[:].rearrange("p a k c -> p (a k c)"),
                            wAH[:].bitcast(F32).rearrange("p a k c -> p (a k c)"), ALU.subtract).then_inc(wA_ok, 1)
            normalise(x_rows(0), zA, z_ok, 1, 2)
            dve.wait_ge(consts, 16 * 6)
            chain(V.tensor_copy(gwH[:], gw_raw[:]), 8)
            V.tensor_tensor(gwL[:], gw_raw[:], gwH[:].bitcast(F32), ALU.subtract).then_inc(gw_ok, 1)
            dve.wait_ge(x_in, 16 * (NB - 1))
            A0 = 8
            A_LINKS = 2 + 5 + 6

            def phase_a(b):
                base = b * A_LINKS + A0

                def low(c):
                    buf = c % 2
                    for k in range(DT):
                        dve.wait_ge(t_hi, 6 * b + 2 * c + k + 1)
                        V.tensor_tensor(tL[:, buf, k], psT[:, buf, k], tH[:, buf, k].bitcast(F32),
                                        ALU.subtract).then_inc(t_split, 1)

                def second_parts(c, base):
                    for m in range(DT):
                        dve.wait_ge(f_taken, 2 + 6 * b + 2 * c + m + 1)
                        chain(V.tensor_tensor(r1[:, m], kf[:, m], parts[:, c, m, 0], ALU.subtract), base + m + 1)
                        V.tensor_copy(parts[:, c, m, 1], r1[:, m]).then_inc(r_ok, 1)

                low(0)
                low(1)
                second_parts(0, base)
                low(2)
                nb = (b + 1) % NB
                variances(x_rows(nb), base + 2)
                second_parts(1, base + 4)
                normalise(x_rows(nb), zA, z_ok, b + 2, base + 6)
                second_parts(2, base + 11)

            with dve.Fori(0, NB) as b:
                phase_a(b)

            B0 = A0 + NB * A_LINKS

            def reduce_tile(t, parity, i):
                dve.wait_ge(m_full, t + 1)
                V.tensor_reduce(mneg[:, parity, i:i + 1], psM[:, i % 2], X_AXIS, ALU.max,
                                negate=True).then_inc(m_free, 1)

            def split_max(n, parity, base):
                dve.wait_ge(mt_full, n + 1)
                src = psO[0:TILES, parity, 0:P]
                chain(V.tensor_copy(msb[:, parity, 0], src), base + 1)
                chain(V.tensor_tensor(mres[:], src, msb[:, parity, 0], ALU.subtract), base + 2)
                chain(V.tensor_copy(msb[:, parity, 1], mres[:]), base + 3)
                V.tensor_tensor(msb[:, parity, 2], mres[:], msb[:, parity, 1], ALU.subtract).then_inc(mt_split, 1)

            dve.wait_ge(ones_k, 1)
            for i in range(TILES):
                reduce_tile(i, 0, i)
            split_max(0, 0, B0)
            for i in range(FIRST):
                reduce_tile(TILES + i, 1, i)
            B1 = B0 + 3
            U_LINKS = 4

            def unit(b, u, last):
                n = 4 * b + u
                links = B1 + U_LINKS * n
                for k in range(KT):
                    for j, off, i in max_tiles(u, k):
                        if exists(last, u + off):
                            reduce_tile(AHEAD + TILES * n + j, (u + off) % 2, i)
                    if k == 3 and exists(last, u + 1):
                        split_max(n + 1, (u + 1) % 2, links)
                dve.wait_ge(ot_full, n + 1)
                dve.wait_ge(o_taken, n + 1)
                o = psO[:, u % 2].rearrange("p (t h v) -> p t h v", t=QT, h=HG)
                used = U_LINKS if exists(last, u + 1) else 1
                chain(V.reciprocal(rden[:], o[:, :, :, DH]), links + used)
                dve.wait_ge(a_st[u % 2], 16 * (2 * b + u // 2 + 1))
                for t in range(QT):
                    ins = V.tensor_tensor(ast[:, u % 2, t].rearrange("p (h d) -> p h d", d=DH), o[:, t, :, 0:DH],
                                          rden[:, t].unsqueeze(2).to_broadcast([P, HG, DH]), ALU.mult)
                    if t == 0:
                        first = ins
                ins.then_inc(o_taken, 1)

            with dve.Fori(0, NB - 1) as b:
                for u in range(NG):
                    unit(b, u, False)
            for u in range(NG):
                unit(NB - 1, u, True)
            C0 = B1 + U_LINKS * UNITS - 3

            R_LINKS = 1 + 2 + 5 + 8

            def r_residual(b, base, first=False):
                if not first:
                    dve.wait_ge(out_st, 16 * b)
                dve.wait_ge(wo_full, b + 1)
                V.tensor_tensor(z2[:], psX[:].rearrange("p a (t d) -> p (a t) d", d=D),
                                bo_s[:].unsqueeze(1).to_broadcast([P, QT, D]), ALU.add).then_inc(dchain, 1)
                dve.wait_ge(dchain, base + 1)
                rows = xs[:, bass.ds(b * QT, QT)]
                chain(V.scalar_tensor_tensor(out=rows, in0=z2[:], scalar=tg[:, 0:1], in1=rows, op0=ALU.mult,
                                             op1=ALU.add), base + 2)
                variances(x_rows(b), base + 2)

            def r_norm(b, base):
                normalise(x_rows(b), z2, z2_ok, NB + 2 + b, base)

            def r_low(b, base):
                for k in range(DT):
                    dve.wait_ge(zt_hi, 2 * b + k + 1)
                    V.tensor_tensor(zTL[:, bass.ds(b % 2, 1), k].rearrange("p a c -> p (a c)"), psX[:, k],
                                    zTH[:, bass.ds(b % 2, 1), k].bitcast(F32).rearrange("p a c -> p (a c)"),
                                    ALU.subtract).then_inc(zt_ok, 1)

            def r_shift(b, base):
                dve.wait_ge(lt_full, b + 1)
                lg = psX[:, 1, 0:QT * NR].rearrange("p (t e) -> p t e", e=NR)
                chain(V.tensor_reduce(small[:, 0], lg, X_AXIS, ALU.max, negate=True), base + 1)
                V.tensor_tensor(pt[:, 0], lg, small[:, 0].unsqueeze(2).to_broadcast([P, QT, NR]),
                                ALU.add).then_inc(d_ok, 1)

            def r_choose(b, base):
                dve.wait_ge(ex_ok, b + 1)
                chain(V.tensor_reduce(small[:, 1], pt[:, 1], X_AXIS, ALU.add), base + 1)
                chain(V.reciprocal(small[:, 2], small[:, 1]), base + 2)
                chain(V.tensor_tensor(pt[:, 2], pt[:, 1], small[:, 2].unsqueeze(2).to_broadcast([P, QT, NR]),
                                      ALU.mult), base + 3)
                for t in range(QT):
                    rows = slice(t * NR, (t + 1) * NR)
                    other = pt[:, 2, t].unsqueeze(1).to_broadcast([P, NR, NR])
                    own = pt[:, 2, t].unsqueeze(2).to_broadcast([P, NR, NR])
                    V.tensor_tensor(cmp[:, 0, rows], other, own, ALU.is_gt)
                    last = V.tensor_tensor(cmp[:, 1, rows], other, own, ALU.is_equal)
                chain(last, base + 4)
                for t in range(QT):
                    rows = slice(t * NR, (t + 1) * NR)
                    last = V.tensor_tensor(cmp[:, 1, rows], cmp[:, 1, rows], trimask[:], ALU.mult)
                chain(last, base + 5)
                chain(V.tensor_tensor(cmp[:, 0], cmp[:, 0], cmp[:, 1], ALU.add), base + 6)
                chain(V.tensor_reduce(rank[:], cmp[:, 0], X_AXIS, ALU.add), base + 7)
                V.scalar_tensor_tensor(out=pt[:, 3].rearrange("p t e -> p (t e)"), in0=rank[:], scalar=1.5,
                                       in1=pt[:, 2].rearrange("p t e -> p (t e)"), op0=ALU.is_lt,
                                       op1=ALU.mult).then_inc(cw_ok, 1)

            router = {1: (r_residual, 0), 2: (r_norm, 4), 3: (r_low, 9), 5: (r_shift, 9), 6: (r_choose, 10)}
            RL = 17

            dve.wait_ge(c_in, 16 * 4)
            dve.wait_ge(cw_ones, 1)
            dve.wait_ge(tanh_ok, 1)
            r_residual(0, C0, first=True)
            for e in (2, 3, 5, 6):
                f, before = router[e]
                f(0, C0 + before)
            C1 = C0 + RL
            E_LINKS = 2 * NR + RL

            def experts(b, last):
                links = C1 + E_LINKS * b
                count = 0

                def low(e, j):
                    dve.wait_ge(gh_ok, 18 * b + 2 * e + j + 1)
                    V.tensor_tensor(gL[:, e % 2, j], g[:, j], gH[:, e % 2, j].bitcast(F32),
                                    ALU.subtract).then_inc(gl_ok, 1)

                for e in range(NE):
                    for j in range(2):
                        q = 18 * b + 2 * e + j
                        dve.wait_ge(sil_ok, q + 1)
                        if e:
                            if j == 0:
                                dve.wait_ge(cwb_ld[e % 2], 16 * (4 * b + (e + 1) // 2))
                            count += 1
                            chain(V.tensor_tensor(sil[:, j], sil[:, j], cwb[:, e % 2], ALU.mult), links + count)
                        V.scalar_tensor_tensor(out=g[:, j], in0=psH[:, j, 1], scalar=b1_s[:, e, 2 + j:3 + j],
                                               in1=sil[:, j], op0=ALU.add, op1=ALU.mult).then_inc(g_ok, 1)
                        if j:
                            low(e, 0)
                        elif e:
                            low(e - 1, 1)
                    if not last and e in router:
                        f, before = router[e]
                        f(b + 1, links + count)
                        count += {1: 4, 2: 5, 3: 0, 5: 1, 6: 7}[e]
                low(NE - 1, 1)
                dve.wait_ge(yt_full, b + 1)
                if last:
                    dve.wait_ge(out_st, 16 * (b + 1))
                V.scalar_tensor_tensor(out=o_s[:], in0=psY[:].rearrange("p a (t d) -> p (a t) d", d=D),
                                       scalar=tg[:, 1:2], in1=xs[:, bass.ds(b * QT, QT)], op0=ALU.mult,
                                       op1=ALU.add).then_inc(y_taken, 1)

            with dve.Fori(0, NB - 1) as b:
                experts(b, False)
            experts(NB - 1, True)

        @block.tensor
        def _(pe):
            mm, tr = nc.tensor.matmul, nc.tensor.transpose

            pe.wait_ge(consts, 16 * 6)

            pe.wait_ge(wA_ok, 1)

            def turn(b, c):
                buf = c % 2
                src = zA if c == 0 else ctxt[:, c - 1]
                if c == 0:
                    pe.wait_ge(z_ok, b + 1)
                else:
                    pe.wait_ge(ctx_ld[c - 1], 16 * (b + 1))
                for k in range(DT):
                    for t in range(QT):
                        last = tr(psT[:, buf, k, t * P:(t + 1) * P], src[:, t, k * P:(k + 1) * P], idn[:])
                    last.then_inc(t_full, 1)

            def project(b, c):
                buf, w = c % 2, min(c, 1)
                pe.wait_ge(t_split, 6 * b + 2 * c + 2)
                terms = ((wAH, tH), (wAL, tH), (wAH, tL))
                if c:
                    for t in range(QT):
                        if t % 2 == 0:
                            pe.wait_ge(v_taken, 4 * b + 2 * (c - 1) + t // 2 + 1)
                        for i, (wt, tt) in enumerate(terms):
                            for k in range(DT):
                                last = mm(psV[:, t // 2, t % 2], tt[:, buf, k, t * P:(t + 1) * P], wt[:, 2, k],
                                          start=(i == 0 and k == 0), stop=(i == 2 and k == DT - 1))
                        if t % 2:
                            last.then_inc(v_full, 1)
                for m in range(DT):
                    pe.wait_ge(f_taken, 6 * b + 2 * c + m + 1)
                    for i, (wt, tt) in enumerate(terms):
                        for k in range(DT):
                            last = mm(psF[:, m], wt[:, w, k, m * P:(m + 1) * P], tt[:, buf, k],
                                      start=(i == 0 and k == 0), stop=(i == 2 and k == DT - 1))
                    last.then_inc(f_full, 1)

            with pe.Fori(0, NB) as b:
                turn(b, 0)
                turn(b, 1)
                project(b, 0)
                turn(b, 2)
                project(b, 1)
                project(b, 2)

            def max_tile(t, slot, i):
                h, qt = divmod(i, QT)
                pe.wait_ge(m_free, t + 1)
                for half in range(2):
                    last = mm(psM[:, i % 2, half * BLK:(half + 1) * BLK],
                              qst[0:SROWS, slot, h, qt * P:(qt + 1) * P],
                              kst[0:SROWS, slot, h, half * BLK:(half + 1) * BLK], start=True, stop=True)
                last.then_inc(m_full, 1)

            def score_tile(s, slot, kt, j):
                pe.wait_ge(e_done, 4 * s + j + 1)
                mm(psS[:, j % 2], kst[:, slot, j, kt * P:(kt + 1) * P], qst[:, slot, j], start=True,
                   stop=True).then_inc(s_full, 1)

            def turn_max(n, parity, tiles, first=False):
                pe.wait_ge(m_free, 2 + tiles)
                if not first:
                    pe.wait_ge(o_taken, n)
                tr(psO[0:TILES, parity, 0:P], mneg[:, parity], idn[:]).then_inc(mt_full, 1)

            pe.wait_ge(ones_k, 1)
            pe.wait_ge(unit_ld[0], 16 * 13)
            for i in range(TILES):
                max_tile(i, 0, i)
            turn_max(0, 0, TILES, first=True)
            pe.wait_ge(unit_ld[1], 16 * 13)
            for i in range(FIRST):
                max_tile(TILES + i, 1, i)
            pe.wait_ge(m_ld[0], 48)
            for s in range(LEAD):
                for j in range(HG):
                    score_tile(s, 0, s, j)

            def values(n, u, k):
                if k == 0:
                    pe.wait_ge(mt_split, n + 1)
                pe.wait_ge(e_done, 2 + 4 * (8 * n + k + 1))
                for j in range(HG):
                    last = mm(psO[j * VW:(j + 1) * VW, u % 2], vt[:, u, k, j * VW:(j + 1) * VW], pr[:, k % 4, j],
                              start=(k == 0), stop=(k == KT - 1), skip_group_check=True)
                last.then_inc(pv_done, 1)

            def unit(b, u, last):
                n = 4 * b + u
                for k in range(KT):
                    nxt, kt = divmod(k + LEAD, KT)
                    slot = (u + nxt) % NG
                    ahead = exists(last, u + nxt)
                    tiles = [(j, off, i) for j, off, i in max_tiles(u, k) if exists(last, u + off)]
                    if ahead and kt == 0:
                        pe.wait_ge(m_ld[slot], 48 * (b + 1 + (u + 1) // NG))

                    def tile(which):
                        for j, off, i in tiles:
                            if j % 2 == which:
                                if off == 2 and i == 0:
                                    pe.wait_ge(unit_ld[(u + 2) % NG], 16 * 13 * (b + 1 + (u + 2) // NG))
                                max_tile(AHEAD + TILES * n + j, (u + off) % NG, i)

                    def score(j):
                        if ahead:
                            score_tile(8 * n + k + LEAD, slot, kt, j)

                    score(0)
                    tile(0)
                    score(1)
                    values(n, u, k)
                    score(2)
                    tile(1)
                    score(3)
                    if k == 3 and exists(last, u + 1):
                        turn_max(n + 1, (u + 1) % 2, AHEAD + TILES * n + REST)
                pe.wait_ge(o_copied, n + 1)
                for t in range(QT):
                    fin = tr(psO[:, u % 2, t * P:(t + 1) * P], osb[:, t * P:(t + 1) * P], idn[:])
                fin.then_inc(ot_full, 1)

            with pe.Fori(0, NB - 1) as b:
                for u in range(NG):
                    unit(b, u, False)
            for u in range(NG):
                unit(NB - 1, u, True)

            def r_attn(b, first=False):
                pe.wait_ge(a_ld, 16 * (b + 1))
                if not first:
                    pe.wait_ge(cwt_ok, b)
                for k in range(DT):
                    for t in range(QT):
                        last = tr(psX[:, k, t * P:(t + 1) * P], a_in[:, t, k * P:(k + 1) * P], idn[:])
                last.then_inc(at_full, 1)

            def r_wo(b):
                pe.wait_ge(at_ok, 2 * b + 2)
                for t in range(QT):
                    for k in range(DT):
                        last = mm(psX[:, t // 2, (t % 2) * D:(t % 2 + 1) * D], aT[:, k, t * P:(t + 1) * P], wo_s[:, k],
                                  start=(k == 0), stop=(k == DT - 1))
                last.then_inc(wo_full, 1)

            def r_turn(b):
                pe.wait_ge(z2_ok, b + 1)
                for k in range(DT):
                    for t in range(QT):
                        last = tr(psX[:, k, t * P:(t + 1) * P], z2[:, t, k * P:(k + 1) * P], idn[:])
                last.then_inc(zt_full, 1)

            def zt(part, b, k):
                return (zTH, zTL)[part][:, bass.ds(b % 2, 1), k].rearrange("p a c -> p (a c)")

            def r_logits(b):
                pe.wait_ge(zt_ok, 2 * b + 2)
                for i, (wt, part) in enumerate(((gwH, 0), (gwL, 0), (gwH, 1))):
                    for k in range(DT):
                        last = mm(psX[0:NR, 0], wt[:, k], zt(part, b, k), start=(i == 0 and k == 0),
                                  stop=(i == 2 and k == DT - 1))
                last.then_inc(lg_full, 1)

            def r_lturn(b):
                pe.wait_ge(lg_sb, b + 1)
                for t in range(QT):
                    last = mm(psX[:, 1, t * NR:(t + 1) * NR], lT[:, t * P:(t + 1) * P], idn[0:NR, 0:NR],
                              start=True, stop=True)
                last.then_inc(lt_full, 1)

            def r_cturn(b):
                pe.wait_ge(cw_ok, b + 1)
                for t in range(QT):
                    last = tr(psX[0:NR, 0, t * P:(t + 1) * P], pt[:, 3, t], idn[:])
                last.then_inc(cwt_full, 1)

            router = {0: r_attn, 1: r_wo, 3: r_turn, 4: r_logits, 5: r_lturn, 7: r_cturn}

            pe.wait_ge(c_in, 16 * 4)
            pe.wait_ge(gw_ok, 1)
            r_attn(0, first=True)
            for e in list(router)[1:]:
                router[e](0)

            def second(b, e, k, stop=False):
                pe.wait_ge(gl_ok, 18 * b + 2 * e + k + 1)
                if e == 0 and k == 0:
                    pe.wait_ge(y_taken, b + 1)
                for m in range(DT):
                    for i, (part, gt) in enumerate(((0, gH), (1, gH), (0, gL))):
                        last = mm(psY[:, m], w2(e, part)[:, k, m * P:(m + 1) * P], gt[:, e % 2, k],
                                  start=(e == 0 and k == 0 and i == 0), stop=(stop and i == 2))
                if k:
                    last.then_inc(w2_done, 1)

            def experts(b, last_b):
                for e in range(NE):
                    if e == 0:
                        pe.wait_ge(zt_ok, 2 * b + 2)
                    pe.wait_ge(w_ok, e + 1)
                    for j in range(2):
                        pe.wait_ge(g_ok, 18 * b + 2 * e + j + 1)
                        for ab in range(2):
                            m = 2 * ab + j
                            for i, (wp, zp) in enumerate(((0, 0), (1, 0), (0, 1))):
                                for k in range(DT):
                                    last = mm(psH[:, j, ab], w1(e, wp)[:, k, m * P:(m + 1) * P], zt(zp, b, k),
                                              start=(i == 0 and k == 0), stop=(i == 2 and k == DT - 1))
                        last.then_inc(h_full, 1)
                        if e == NE - 1 and j == 0:
                            second(b, e - 1, 0)
                            second(b, e - 1, 1)
                    if 0 < e < NE - 1:
                        second(b, e - 1, 0)
                        second(b, e - 1, 1)
                    if not last_b and e in router:
                        router[e](b + 1)
                pe.wait_ge(cwt_ok, b + 1)
                second(b, NE - 1, 0)
                for m in range(DT):
                    mm(psY[:, m], b2_s[:, m * P:(m + 1) * P], cw_of(b), start=False, stop=False)
                second(b, NE - 1, 1, stop=True)
                pe.wait_ge(y_copied, 2 * b + 2)
                for t in range(QT):
                    for m in range(DT):
                        last = tr(psY[:, t // 2, (t % 2) * D + m * P:(t % 2) * D + (m + 1) * P],
                                  yT[:, m, t * P:(t + 1) * P], idn[:])
                last.then_inc(yt_full, 1)

            with pe.Fori(0, NB - 1) as b:
                experts(b, False)
            experts(NB - 1, True)


def kernel(x, ctx_1024, g_xattn, g_ffn, L0_xattn_Wq, L0_xattn_bq, L0_xattn_Wk, L0_xattn_bk, L0_xattn_Wv,
           L0_xattn_bv, L0_xattn_Wo, L0_xattn_bo, L0_ffn_gate_w, L0_ffn_gate_b, L0_ffn_sw1, L0_ffn_sb1,
           L0_ffn_sw2, L0_ffn_sb2, L0_ffn_rw1, L0_ffn_rb1, L0_ffn_rw2, L0_ffn_rb2):
    import numpy as np
    import concourse.bacc as bacc
    from concourse.bass_utils import run_bass_kernel_spmd

    def rows(w):
        w = np.asarray(w)
        return w.reshape(w.shape[0] // P, P, w.shape[1]).transpose(1, 0, 2)

    def spread(v, n=P):
        return np.broadcast_to(np.asarray(v), (n, np.asarray(v).shape[0]))

    w1 = np.concatenate([np.asarray(L0_ffn_sw1), np.asarray(L0_ffn_rw1)])
    w2 = np.concatenate([np.asarray(L0_ffn_sw2), np.asarray(L0_ffn_rw2)])
    b1 = np.concatenate([np.asarray(L0_ffn_sb1), np.asarray(L0_ffn_rb1)])
    arrays = {
        "x": x, "ctx": ctx_1024,
        "gates": spread(np.concatenate([np.asarray(g_xattn), np.asarray(g_ffn)])),
        "wqkv": np.stack([rows(np.asarray(w).T) for w in (L0_xattn_Wq, L0_xattn_Wk, L0_xattn_Wv)], axis=1),
        "bqkv": np.stack([np.asarray(v).reshape(DT, P).T for v in (L0_xattn_bq, L0_xattn_bk, L0_xattn_bv)], axis=1),
        "wo": rows(np.asarray(L0_xattn_Wo).T), "bo": spread(L0_xattn_bo),
        "gate_w": rows(L0_ffn_gate_w), "gate_b": np.asarray(L0_ffn_gate_b).reshape(NR, 1),
        "wexp": np.stack([np.concatenate([rows(a).reshape(P, -1), rows(c).reshape(P, -1)], axis=1)
                          for a, c in zip(w1, w2)]),
        "b1": b1.reshape(NE, 4, P).transpose(2, 0, 1),
        "b2": np.concatenate([np.asarray(L0_ffn_rb2), np.asarray(L0_ffn_sb2)]),
        "ident": np.eye(P, dtype=np.float32),
        "tri": np.broadcast_to(np.tril(np.ones((NR, NR), np.float32), -1), (P, NR, NR)),
    }
    arrays = {k: np.ascontiguousarray(v) for k, v in arrays.items()}
    nc = bacc.Bacc("TRN2", target_bir_lowering=False, num_devices=1)
    args = [nc.dram_tensor(k, v.shape, mybir.dt.from_np(v.dtype), kind="ExternalInput").ap()
            for k, v in arrays.items()]
    out = nc.dram_tensor("out", (NB, NQ, D), F32, kind="ExternalOutput").ap()
    build(nc, *args, out)
    r = run_bass_kernel_spmd(nc, [arrays], core_ids=[0])
    return r.results[0]["out"]
```

```python
import math
from contextlib import ExitStack

import concourse.bass as bass
from concourse import mybir

F32 = mybir.dt.float32
F32R = mybir.dt.float32r
BF16 = mybir.dt.bfloat16
ALU = mybir.AluOpType
ACT = mybir.ActivationFunctionType
X_AXIS = mybir.AxisListType.X

P = 128
NB, NQ, NK, D = 4, 512, 1024, 256
NH, DH = 16, 16
DT = D // P
QT = NQ // P
KT = NK // P
HG = 4
NG = NH // HG
UNITS = NB * NG
TERMS = ((0, 0), (0, 1), (1, 0), (1, 1), (0, 2), (2, 0))
SROWS = len(TERMS) * DH
MROWS = SROWS + 3
VW = 32
NE = 9
NR = NE - 1
FF = 256
EARLY = 3
WCOLS = DT * 2 * FF + DT * D
BLK = 512
EPS = 1e-5
SCALE = 1.0 / DH ** 0.5


def build(nc, x, ctx_in, gates, wqkv, bqkv, wo, bo, gate_w, gate_b, wexp, b1, b2, ident, tri, out):
    dram = lambda name, shape, dt: nc.dram_tensor(name, shape, dt, kind="Internal").ap()
    q_parts = dram("q_parts", [NB, 3, D, NQ], BF16)
    k_parts = dram("k_parts", [NB, 3, D, NK], BF16)
    v_pad = dram("v_pad", [NB, KT, P, NH * VW], F32)
    attn = dram("attn", [NB, P, QT, D], F32)
    cw_rows = dram("cw_rows", [NR, NB * NQ], F32)

    with ExitStack() as es:
        sb = lambda name, shape, dt=F32, st=es: st.enter_context(nc.sbuf_tensor(name, shape, dt))
        ps = lambda name, shape, st=es: st.enter_context(nc.psum_tensor(name, shape, F32))
        sem = lambda name: es.enter_context(nc.semaphore(name))

        xs = sb("xs", [P, NB * QT, D])
        idn = sb("idn", [P, P])
        eW1H = sb("eW1H", [P, EARLY, DT, 2 * FF], F32R)
        eW1L = sb("eW1L", [P, EARLY, DT, 2 * FF], F32R)
        eW2H = sb("eW2H", [P, EARLY, DT, D], F32R)
        eW2L = sb("eW2L", [P, EARLY, DT, D], F32R)
        wraw = sb("wraw", [P, 2, WCOLS])
        trimask = sb("trimask", [P, NR, NR])
        tg_in = sb("tg_in", [P, 2])
        tg = sb("tg", [P, 2])
        bq_s = sb("bq_s", [P, 3, DT])
        gb_s = sb("gb_s", [NR, 1])
        gw_raw = sb("gw_raw", [P, DT, NR])
        gwH = sb("gwH", [P, DT, NR], F32R)
        gwL = sb("gwL", [P, DT, NR], F32R)
        blank = sb("blank", [P, 1])
        stats = sb("stats", [P, QT, 6])
        mv = sb("mv", [P, QT, 2])
        veps = sb("veps", [P, QT])
        std = sb("std", [P, QT])
        rstd = sb("rstd", [P, QT])
        nt = sb("nt", [P, QT])

        sa = ExitStack()
        a_names = [("parts", [P, 3, DT, 3, BLK], BF16), ("vst", [P, 4, 2, NH, VW], F32), ("kf", [P, 2, BLK], F32),
                   ("wA_raw", [P, 3, DT, D], F32), ("ctxt", [P, 2, QT, D], F32), ("zA", [P, QT, D], F32),
                   ("wAH", [P, 3, DT, D], F32R), ("wAL", [P, 3, DT, D], F32R), ("tH", [P, 3, DT, BLK], F32R),
                   ("tL", [P, 3, DT, BLK], F32R)]
        parts, vst, kf, wA_raw, ctxt, zA, wAH, wAL, tH, tL = (sb(*a, sa) for a in a_names)
        sa.close()
        nbytes = lambda shape, dt: (2 if dt == BF16 else 4) * math.prod(shape[1:])
        z_names = [("zTH", [P, 2, DT, BLK], F32R), ("zTL", [P, 2, DT, BLK], F32R), ("a_in", [P, QT, D], F32),
                   ("aT", [P, DT, BLK], F32), ("wo_s", [P, DT, D], F32), ("bo_s", [P, D], F32),
                   ("z2", [P, QT, D], F32), ("pt", [P, 4, QT, NR], F32), ("small", [P, 3, QT], F32),
                   ("cmp", [P, 2, QT * NR, NR], F32), ("rank", [P, QT * NR], F32), ("cwT", [NE, 2, BLK], F32),
                   ("b1_s", [P, NE, 4], F32), ("b2_s", [NE, D], F32)]
        zTH, zTL, a_in, aT, wo_s, bo_s, z2, pt, small, cmp, rank, cwT, b1_s, b2_s = (sb(*a) for a in z_names)
        lT = cmp[0:NR].rearrange("e a r n -> e (a r n)")
        sB = ExitStack()
        b_names = [("pr", [P, 4, HG, NQ], F32), ("vt", [P, NG, KT, HG * VW], F32), ("osb", [P, NQ], F32),
                   ("rden", [P, QT, HG], F32), ("ast", [P, 2, QT, HG * DH], F32)]
        pr, vt, osb, rden, ast = (sb(*b, sB) for b in b_names)
        over = sum(nbytes(a, t) for _, a, t in a_names) - sum(nbytes(a, t) for _, a, t in z_names + b_names)
        if over > -64:
            sb("gap", [P, over // 4 + 32], F32, sB)
        mneg = sb("mneg", [P, 2, HG * QT], F32, sB)
        msb = sb("msb", [HG * QT, 2, 3, P], BF16, sB)
        mres = sb("mres", [HG * QT, P], F32, sB)
        kst = sb("kst", [MROWS, NG, HG, NK], BF16, sB)
        qst = sb("qst", [MROWS, NG, HG, NQ], BF16, sB)
        sB.close()
        lW1H = sb("lW1H", [P, NE - EARLY, DT, 2 * FF], F32R)
        lW1L = sb("lW1L", [P, NE - EARLY, DT, 2 * FF], F32R)
        lW2H = sb("lW2H", [P, NE - EARLY, DT, D], F32R)
        lW2L = sb("lW2L", [P, NE - EARLY, DT, D], F32R)
        cwb = sb("cwb", [P, 2, BLK])
        sil = sb("sil", [P, 2, BLK])
        g = sb("g", [P, 2, BLK])
        gH = sb("gH", [P, 2, 2, BLK], F32R)
        gL = sb("gL", [P, 2, 2, BLK], F32R)
        yT = aT
        o_s = z2

        pa = ExitStack()
        psT = ps("psT", [P, DT, BLK], pa)
        psF = ps("psF", [P, DT, BLK], pa)
        psV = ps("psV", [P, 2, 2, D], pa)
        pa.close()
        pb = ExitStack()
        psM = ps("psM", [P, 2, NK], pb)
        psS = ps("psS", [P, 2, NQ], pb)
        psO = ps("psO", [P, 2, NQ], pb)
        pb.close()
        psX = ps("psX", [P, 2, BLK])
        psH = ps("psH", [P, 2, 2, BLK])
        psY = ps("psY", [P, 2, BLK])
        psE = psO[:].rearrange("p a t -> p (a t)")

        consts = sem("consts"); idn_in = sem("idn_in")
        wA_in = sem("wA_in")
        x0_in = sem("x0_in"); x_in = sem("x_in")
        ctx_ld = [sem("ctx_in0"), sem("ctx_in1")]
        c_in = sem("c_in"); v_ld = [sem(f"unit_v_in{s}") for s in range(NG)]
        wA_hi = sem("wA_hi"); wA_ok = sem("wA_ok")
        gw_ok = sem("gw_ok")
        dchain = sem("dve_chain")
        tanh_ok = sem("tanh_ok")
        var_ok = sem("var_ok"); std_ok = sem("std_ok"); z_ok = sem("z_ok")
        t_full = sem("t_full"); t_hi = sem("t_hi"); t_split = sem("t_split")
        f_full = sem("f_full"); f_taken = sem("f_taken"); r_ok = sem("r_ok"); k_ok = sem("k_parts_ok")
        v_full = sem("v_full"); v_taken = sem("v_taken")
        qk_st = [sem(f"parts_stored{c}") for c in range(3)]
        v_st = [sem(f"v_stored{s}") for s in range(4)]
        pads = sem("pads"); ones_k = sem("ones_k"); cw_ones = sem("cw_ones")
        unit_ld = [sem(f"unit_in{s}") for s in range(NG)]
        m_ld = [sem(f"max_in{s}") for s in range(NG)]
        m_full = sem("m_full"); m_free = sem("m_free")
        mt_full = sem("mt_full"); mt_split = sem("mt_split")
        s_full = sem("s_full"); e_done = sem("exp_done")
        pv_done = sem("pv_done")
        o_copied = sem("o_copied"); ot_full = sem("ot_full"); o_taken = sem("o_taken")
        a_st = [sem("a_stored0"), sem("a_stored1")]
        raw_ld = [sem("raw_in0"), sem("raw_in1")]
        pool_c = sem("pool_chain"); w_ok = sem("w_ok")
        a_ld = sem("a_in"); at_full = sem("at_full"); at_ok = sem("at_ok")
        wo_full = sem("wo_full"); z2_ok = sem("z2_ok"); zt_full = sem("zt_full")
        zt_hi = sem("zt_hi"); zt_ok = sem("zt_ok")
        lg_full = sem("lg_full"); lg_sb = sem("lg_sb"); lt_full = sem("lt_full")
        d_ok = sem("d_ok"); ex_ok = sem("ex_ok"); cw_ok = sem("cw_ok")
        cwt_full = sem("cwt_full"); cwt_ok = sem("cwt_ok"); cw_st = sem("cw_stored")
        cwb_ld = [sem("cwb_in0"), sem("cwb_in1")]
        h_full = sem("h_full"); sil_ok = sem("sil_ok"); g_ok = sem("g_ok")
        gh_ok = sem("gh_ok"); gl_ok = sem("gl_ok"); w2_done = sem("w2_done")
        y_copied = sem("y_copied"); yt_full = sem("yt_full")
        y_taken = sem("y_taken"); out_st = sem("out_stored")

        def w1(e, part):
            return (eW1H, eW1L)[part][:, e] if e < EARLY else (lW1H, lW1L)[part][:, e - EARLY]

        def w2(e, part):
            return (eW2H, eW2L)[part][:, e] if e < EARLY else (lW2H, lW2L)[part][:, e - EARLY]

        def cw_of(b):
            return cwT[:, bass.ds(b % 2, 1)].rearrange("e a t -> e (a t)")

        TILES = HG * QT
        FIRST = 10
        REST = TILES - FIRST
        AHEAD = TILES + FIRST
        LEAD = 2

        EARLY_PLACES = [(NB - 2, 1, place) for place in ("v1", "v3", "f0", "f1")]
        EARLY_PLACES += [(NB - 2, 2, place) for place in ("f0", "f1")]
        EARLY_PLACES += [(NB - 1, c, place) for c in range(2) for place in ("v1", "v2", "v3", "f0", "f1")]

        def early_tiles(b, c, place):
            if not isinstance(b, int):
                return []
            return [i for i, where in enumerate(EARLY_PLACES) if where == (b, c, place)]

        def max_tiles(u, step):
            for j in (2 * step, 2 * step + 1):
                yield (j, 1, FIRST + j) if j < REST else (j, 2, j - REST)

        def exists(last, u):
            return not last or u < NG

        block = es.enter_context(nc.Block())

        @block.sync
        def _(sp):
            sp.dma_start(ctxt[:, 0], ctx_in[0, 0:BLK].rearrange("(t p) d -> p t d", p=P)).then_inc(ctx_ld[0], 16)
            sp.dma_start(idn[:], ident).then_inc(idn_in, 16)
            sp.dma_start(wA_raw[:], wqkv).then_inc(wA_in, 16)
            sp.dma_start(ctxt[:, 1], ctx_in[0, BLK:2 * BLK].rearrange("(t p) d -> p t d", p=P)).then_inc(ctx_ld[1], 16)
            sp.dma_start(xs[:, 0:QT, :], x[0].rearrange("(t p) d -> p t d", p=P)).then_inc(x0_in, 16)
            sp.dma_start(tg_in[:], gates).then_inc(consts, 16)
            sp.dma_start(bq_s[:], bqkv).then_inc(consts, 16)
            sp.dma_start(gw_raw[:], gate_w).then_inc(consts, 16)
            sp.dma_start(gb_s[:], gate_b).then_inc(consts, 16)
            sp.dma_start(trimask[:], tri).then_inc(consts, 16)
            for b in range(1, NB):
                sp.dma_start(xs[:, b * QT:(b + 1) * QT, :],
                             x[b].rearrange("(t p) d -> p t d", p=P)).then_inc(x_in, 16)

            def stores(b, load_next, before_last=None):
                if load_next:
                    for h in range(2):
                        sp.wait_ge(t_full, 6 * b + 2 * h + 2)
                        sp.dma_start(ctxt[:, h], ctx_in[b + 1, h * BLK:(h + 1) * BLK].rearrange(
                            "(t p) d -> p t d", p=P)).then_inc(ctx_ld[h], 16)
                for c in range(3):
                    if c == 2 and before_last:
                        before_last()
                    if c < 2:
                        for s in range(2):
                            slot = 2 * c + s
                            sp.wait_ge(v_taken, 2 + 4 * b + slot + 1)
                            sp.dma_start(v_pad[b, 2 * slot:2 * slot + 2].rearrange("t p c -> p t c"),
                                         vst[:, slot].rearrange("p t h v -> p t (h v)")).then_inc(v_st[slot], 16)
                    for m in range(DT):
                        sp.wait_ge(k_ok, 2 + 6 * b + 2 * c + m + 1)
                        dst = q_parts[b] if c == 2 else k_parts[b, :, :, c * BLK:(c + 1) * BLK]
                        sp.dma_start(dst[:, m * P:(m + 1) * P, :].rearrange("s p t -> p s t"),
                                     parts[:, c, m]).then_inc(qk_st[c], 16)

            def load_unit(b, u):
                for t, (qp, kp) in enumerate(TERMS):
                    rows = slice(t * DH, (t + 1) * DH)
                    heads = slice(u * HG * DH, (u + 1) * HG * DH)
                    sp.dma_start(qst[rows, u], q_parts[b, qp, heads, :].rearrange("(h d) t -> d h t", d=DH)
                                 ).then_inc(unit_ld[u], 16)
                    sp.dma_start(kst[rows, u], k_parts[b, kp, heads, :].rearrange("(h d) t -> d h t", d=DH)
                                 ).then_inc(unit_ld[u], 16)

            def load_values(b, u):
                sp.dma_start(vt[:, u], v_pad[b, :, :, u * HG * VW:(u + 1) * HG * VW].rearrange("k p c -> p k c")
                             ).then_inc(v_ld[u], 16)

            def load_max(b, u):
                for s in range(3):
                    sp.dma_start(qst[SROWS + s:SROWS + s + 1, u], msb[:, u % 2, s, :]).then_inc(m_ld[u], 16)

            def first_unit():
                for c in range(3):
                    sp.wait_ge(qk_st[c], 32 + 32)
                load_unit(0, 0)

            stores(0, True)
            stores(1, True, first_unit)
            for b in range(2, NB - 1):
                stores(b, True)
            load_unit(0, 1)

            def first_max():
                sp.wait_ge(mt_split, 1)
                load_max(0, 0)

            stores(NB - 1, False, first_max)
            sp.wait_ge(f_full, 6 + 6 * NB)
            for s in range(4):
                sp.wait_ge(v_st[s], 16 + 16)
            load_values(0, 0)
            load_values(0, 1)
            load_unit(0, 2)
            load_values(0, 2)
            load_unit(0, 3)
            load_values(0, 3)
            for c in range(3):
                sp.wait_ge(qk_st[c], 32 + 32 * NB)
            for s in range(4):
                sp.wait_ge(v_st[s], 16 + 16 * NB)

            def unit_dmas(b, u, last):
                if exists(last, u + 1):
                    sp.wait_ge(mt_split, 4 * b + u + 2)
                    load_max(b, (u + 1) % NG)
                if not last:
                    sp.wait_ge(pv_done, 4 + KT * (4 * b + u + 1))
                    load_unit(b + 1, u)
                    load_values(b + 1, u)
                sp.wait_ge(o_taken, 4 * b + u + 2)
                sp.dma_start(attn[b, :, :, u * HG * DH:(u + 1) * HG * DH], ast[:, u % 2]).then_inc(a_st[u % 2], 16)

            with sp.Fori(0, NB - 1) as b:
                for u in range(NG):
                    unit_dmas(b, u, False)
            for s in range(2):
                sp.wait_ge(a_st[s], 16 + 16 * (UNITS - NG) // 2)
            sp.dma_start(a_in[:], attn[0]).then_inc(a_ld, 16)
            sp.dma_start(wo_s[:], wo).then_inc(c_in, 16)
            sp.dma_start(bo_s[:], bo).then_inc(c_in, 16)
            sp.dma_start(b1_s[:], b1).then_inc(c_in, 16)
            sp.dma_start(b2_s[:], b2).then_inc(c_in, 16)
            for u in range(NG):
                unit_dmas(NB - 1, u, True)
            for s in range(2):
                sp.wait_ge(a_st[s], 16 + 16 * UNITS // 2)

            def store_weights(b):
                sp.wait_ge(cwt_ok, b + 1)
                cols = bass.ds(b * BLK, BLK)
                sp.dma_start(cw_rows[:, cols], cw_of(b)[0:NR]).then_inc(cw_st, 16)

            def broadcast_weights(b, e):
                sp.wait_ge(g_ok, 2 + 18 * b + (2 * (e - 1) if e > 2 else 0))
                row = cw_rows[e - 1:e, bass.ds(b * BLK, BLK)]
                sp.dma_start(cwb[:, e % 2, :], row.to_broadcast([P, BLK])).then_inc(cwb_ld[e % 2], 16)

            def expert_dmas(b, last):
                for e in range(3, NE):
                    broadcast_weights(b, e)
                if not last:
                    sp.wait_ge(at_full, b + 2)
                    sp.dma_start(a_in[:], attn[(b + 2) % NB]).then_inc(a_ld, 16)
                    store_weights(b + 1)
                    sp.wait_ge(cw_st, 16 * (b + 2))
                    for e in (1, 2):
                        broadcast_weights(b + 1, e)
                sp.wait_ge(y_taken, b + 2)
                sp.dma_start(out[b].rearrange("(t p) d -> p t d", p=P), o_s[:]).then_inc(out_st, 16)

            sp.wait_ge(at_full, 1)
            sp.dma_start(a_in[:], attn[1]).then_inc(a_ld, 16)
            store_weights(0)
            sp.wait_ge(ot_full, UNITS)
            sp.wait_ge(cw_st, 16)
            for e in (1, 2):
                broadcast_weights(0, e)
            with sp.Fori(0, NB - 1) as b:
                expert_dmas(b, False)
            expert_dmas(NB - 1, True)
            sp.wait_ge(out_st, 16 + 16 * NB)
            sp.wait_ge(a_ld, 16 * (NB + 1))

        @block.gpsimd
        def _(pool):
            nc.gpsimd.dma_start(wraw[:, 0], wexp[0]).then_inc(raw_ld[0], 16)
            nc.gpsimd.dma_start(wraw[:, 1], wexp[1]).then_inc(raw_ld[1], 16)
            for s, n in ((f_full, 6), (t_split, 2), (f_taken, 2), (k_ok, 2), (v_taken, 2), (m_free, 2), (e_done, 2),
                         (pv_done, 4), (o_taken, 1), (g_ok, 2), (w2_done, 2), (y_taken, 1), (out_st, 16)):
                pool.sem_inc(s, n)
            for c in range(3):
                pool.sem_inc(qk_st[c], 32)
            for s in range(4):
                pool.sem_inc(v_st[s], 16)
            for s in range(2):
                pool.sem_inc(a_st[s], 16)
            nc.gpsimd.memset(kst[SROWS:MROWS], 1.0).then_inc(ones_k, 1)
            pool.wait_ge(ones_k, 1)
            nc.gpsimd.memset(vst[:, :, :, :, DH:VW].rearrange("p a b h v -> p (a b h) v"), 0.0).then_inc(pool_c, 1)
            pool.wait_ge(pool_c, 1)
            nc.gpsimd.memset(vst[:, :, :, :, DH:DH + 1].rearrange("p a b h v -> p (a b h) v"), 1.0).then_inc(pads, 1)

            def third_parts(b):
                for c in range(3):
                    for m in range(DT):
                        pool.wait_ge(r_ok, 6 * b + 2 * c + m + 1)
                        nc.gpsimd.tensor_tensor(parts[:, c, m, 2], kf[:, m], parts[:, c, m, 1],
                                                ALU.subtract).then_inc(k_ok, 1)

            with pool.Fori(0, NB) as b:
                third_parts(b)

            for c in range(3):
                pool.wait_ge(qk_st[c], 32 + 32 * NB)
            for s in range(4):
                pool.wait_ge(v_st[s], 16 + 16 * NB)
            pool.wait_ge(f_full, 6 + 6 * NB)
            nc.gpsimd.memset(cwT[:], 1.0).then_inc(cw_ones, 1)
            pool.wait_ge(cw_ones, 1)

            def prepare(e, r, outs):
                nw1 = DT * 2 * FF
                base = 1 + 3 * e
                hi1, lo1, hi2, lo2 = outs
                raw1, raw2 = wraw[:, r, 0:nw1], wraw[:, r, nw1:WCOLS]
                nc.gpsimd.tensor_copy(hi1, raw1).then_inc(pool_c, 1)
                pool.wait_ge(pool_c, base + 1)
                nc.gpsimd.tensor_tensor(lo1, raw1, hi1.bitcast(F32), ALU.subtract).then_inc(pool_c, 1)
                nc.gpsimd.tensor_copy(hi2, raw2).then_inc(pool_c, 1)
                pool.wait_ge(pool_c, base + 3)
                nc.gpsimd.tensor_tensor(lo2, raw2, hi2.bitcast(F32), ALU.subtract).then_inc(w_ok, 1)
                pool.wait_ge(w_ok, e + 1)

            def flat(tensors, e):
                return tuple(t[:, bass.ds(e, 1)].rearrange("p a k c -> p (a k c)") for t in tensors)

            for e in range(EARLY):
                r = e % 2
                pool.wait_ge(raw_ld[r], 16 * (e // 2 + 1))
                prepare(e, r, flat((eW1H, eW1L, eW2H, eW2L), e))
                nc.gpsimd.dma_start(wraw[:, r], wexp[e + 2]).then_inc(raw_ld[r], 16)
            pool.wait_ge(ot_full, UNITS)
            for s in range(2):
                pool.wait_ge(a_st[s], 16 + 16 * UNITS // 2)
            for e in range(EARLY, NE):
                r = e % 2
                pool.wait_ge(raw_ld[r], 16 * (e // 2 + 1))
                prepare(e, r, flat((lW1H, lW1L, lW2H, lW2L), e - EARLY))
                if e + 2 < NE:
                    nc.gpsimd.dma_start(wraw[:, r], wexp[e + 2]).then_inc(raw_ld[r], 16)

        @block.scalar
        def _(act):
            def sqrt_of(n):
                act.wait_ge(var_ok, n)
                nc.scalar.activation(std[:], veps[:], ACT.Sqrt).then_inc(std_ok, 1)

            act.wait_ge(wA_in, 16)
            nc.scalar.copy(wAH[:].rearrange("p a k c -> p (a k c)"),
                           wA_raw[:].rearrange("p a k c -> p (a k c)")).then_inc(wA_hi, 1)

            def high(b, c):
                act.wait_ge(f_full, 6 * b + 2 * c + 2)
                for k in range(DT):
                    act.wait_ge(t_full, 6 * b + 2 * c + k + 1)
                    nc.scalar.copy(tH[:, c, k], psT[:, k]).then_inc(t_hi, 1)

            def biased(b, c):
                for m in range(DT):
                    i = 6 * b + 2 * c + m
                    act.wait_ge(f_full, 6 + i + 1)
                    act.wait_ge(k_ok, i + 1)
                    act.wait_ge(qk_st[c], 32 * (b + 1))
                    bias = bq_s[:, 0 if c == 2 else 1, m:m + 1]
                    nc.scalar.activation(kf[:, m], psF[:, m], ACT.Identity, bias=bias)
                    nc.scalar.activation(parts[:, c, m, 0], psF[:, m], ACT.Identity,
                                         bias=bias).then_inc(f_taken, 1)

            def values(b, c):
                for s in range(2):
                    slot = 2 * c + s
                    act.wait_ge(v_full, 4 * b + slot + 1)
                    act.wait_ge(v_st[slot], 16 * (b + 1))
                    nc.scalar.copy(vst[:, slot, :, :, 0:DH], psV[:, s].rearrange("p t (h d) -> p t h d", d=DH)
                                   ).then_inc(v_taken, 1)

            def phase_a(b, last):
                values(b, 0)
                biased(b, 0)
                high(b, 2)
                if not last:
                    sqrt_of(b + 2)
                values(b, 1)
                biased(b, 1)
                if not last:
                    high(b + 1, 0)
                biased(b, 2)
                if not last:
                    high(b + 1, 1)

            high(0, 0)
            high(0, 1)
            sqrt_of(1)
            act.wait_ge(consts, 16 * 5)
            act.wait_ge(pads, 1)
            with act.Fori(0, NB - 1) as b:
                phase_a(b, False)
            phase_a(NB - 1, True)

            nc.scalar.activation(tg[:], tg_in[:], ACT.Tanh).then_inc(tanh_ok, 1)

            def exponentials(s, slot, j):
                if j == 0:
                    act.wait_ge(pv_done, s + 1)
                act.wait_ge(s_full, 4 * s + j + 1)
                nc.scalar.activation(pr[:, slot, j], psS[:, j % 2], ACT.Exp, scale=SCALE).then_inc(e_done, 1)

            for s in range(LEAD):
                for j in range(HG):
                    exponentials(s, s % 4, j)

            def unit_exps(b, u, last):
                n = 4 * b + u
                for k in range(KT):
                    ahead = exists(last, u + (k + LEAD) // KT)
                    for j in range(HG):
                        if ahead:
                            exponentials(8 * n + k + LEAD, (k + LEAD) % 4, j)
                        if k == KT - 1 and j == 1:
                            act.wait_ge(pv_done, 4 + KT * (n + 1))
                            nc.scalar.copy(osb[:], psO[:, u % 2]).then_inc(o_copied, 1)
                    if last and u == NG - 1 and k in router:
                        router[k](0)

            def r_attn(b):
                act.wait_ge(at_full, b + 1)
                for k in range(DT):
                    nc.scalar.activation(aT[:, k], psX[:, k], ACT.Identity,
                                         bias=bq_s[:, 2, k:k + 1]).then_inc(at_ok, 1)

            def r_sqrt(b):
                sqrt_of(NB + 1 + b)

            def r_high(b):
                act.wait_ge(zt_full, b + 1)
                for k in range(DT):
                    nc.scalar.copy(zTH[:, bass.ds(b % 2, 1), k].rearrange("p a c -> p (a c)"), psX[:, k]).then_inc(zt_hi, 1)

            def r_logits(b):
                act.wait_ge(lg_full, b + 1)
                nc.scalar.activation(lT[:], psX[0:NR, 0], ACT.Identity, bias=gb_s[:, 0:1]).then_inc(lg_sb, 1)

            def r_exp(b):
                act.wait_ge(d_ok, b + 1)
                nc.scalar.activation(pt[:, 1], pt[:, 0], ACT.Exp).then_inc(ex_ok, 1)

            def r_cwt(b):
                act.wait_ge(cwt_full, b + 1)
                nc.scalar.copy(cw_of(b)[0:NR], psX[0:NR, 0]).then_inc(cwt_ok, 1)

            router = {0: r_attn, 2: r_sqrt, 3: r_high, 4: r_logits, 5: r_exp, 7: r_cwt}

            with act.Fori(0, NB - 1) as b:
                for u in range(NG):
                    unit_exps(b, u, False)
            for u in range(NG):
                if u == NG - 1:
                    act.wait_ge(c_in, 16 * 4)
                    act.wait_ge(cw_ones, 1)
                unit_exps(NB - 1, u, True)

            def silu(b, e, j):
                act.wait_ge(h_full, 18 * b + 2 * e + j + 1)
                nc.scalar.activation(sil[:, j], psH[:, j, 0], ACT.Silu, bias=b1_s[:, e, j:j + 1]).then_inc(sil_ok, 1)

            def gated_high(b, e, j):
                if j == 0:
                    act.wait_ge(w2_done, 9 * b + (e + 1 if e else 2))
                act.wait_ge(g_ok, 2 + 18 * b + 2 * e + j + 1)
                nc.scalar.copy(gH[:, e % 2, j], g[:, j]).then_inc(gh_ok, 1)

            def sum_copy(b):
                act.wait_ge(w2_done, 2 + 9 * (b + 1))
                for m in range(DT):
                    nc.scalar.copy(yT[:, m], psY[:, m]).then_inc(y_copied, 1)

            for s in range(2):
                act.wait_ge(a_st[s], 16 + 16 * UNITS // 2)
            for j in range(2):
                silu(0, 0, j)
                gated_high(0, 0, j)

            def experts(b, last):
                for e in range(1, NE):
                    for j in range(2):
                        silu(b, e, j)
                        gated_high(b, e, j)
                    if not last and e - 1 in router:
                        router[e - 1](b + 1)
                if not last:
                    silu(b + 1, 0, 0)
                sum_copy(b)
                if not last:
                    gated_high(b + 1, 0, 0)
                    silu(b + 1, 0, 1)
                    gated_high(b + 1, 0, 1)

            with act.Fori(0, NB - 1) as b:
                experts(b, False)
            experts(NB - 1, True)

        @block.vector
        def _(dve):
            V = nc.vector
            def chain(ins, value):
                ins.then_inc(dchain, 1)
                dve.wait_ge(dchain, value)

            NORM1, NORM2 = 3, 7

            def variances(rows, base):
                V.memset(blank[:], 0.0)
                for t in range(QT):
                    last = V.bn_stats(stats[:, t], rows(t))
                chain(last, base + 1)
                V.memset(blank[:], 0.0)
                for t in range(QT):
                    last = V.bn_aggr(mv[:, t], stats[:, t])
                chain(last, base + 2)
                V.tensor_scalar(veps[:], mv[:, :, 1], EPS, None, ALU.add).then_inc(var_ok, 1)

            def normalise(rows, dst, done, nth, base):
                dve.wait_ge(std_ok, nth)
                chain(V.reciprocal(rstd[:], std[:]), base + 1)
                chain(V.tensor_tensor(nt[:], rstd[:], rstd[:], ALU.mult), base + 2)
                chain(V.tensor_tensor(nt[:], nt[:], veps[:], ALU.mult), base + 3)
                chain(V.tensor_scalar(nt[:], nt[:], -0.5, 1.5, ALU.mult, ALU.add), base + 4)
                chain(V.tensor_tensor(rstd[:], rstd[:], nt[:], ALU.mult), base + 5)
                for t in range(QT):
                    last = V.tensor_scalar(dst[:, t], rows(t), mv[:, t, 0:1], rstd[:, t:t + 1],
                                           ALU.subtract, ALU.mult)
                last.then_inc(done, 1)

            def x_rows(b):
                return lambda t: xs[:, bass.ds(b * QT + t, 1)].rearrange("p a d -> p (a d)")

            def low(b, c):
                for k in range(DT):
                    dve.wait_ge(t_hi, 6 * b + 2 * c + k + 1)
                    V.tensor_tensor(tL[:, c, k], psT[:, k], tH[:, c, k].bitcast(F32),
                                    ALU.subtract).then_inc(t_split, 1)

            def split_max(n, parity, base):
                dve.wait_ge(mt_full, n + 1)
                src = psO[0:TILES, parity, 0:P]
                chain(V.tensor_copy(msb[:, parity, 0], src), base + 1)
                chain(V.tensor_tensor(mres[:], src, msb[:, parity, 0], ALU.subtract), base + 2)
                chain(V.tensor_copy(msb[:, parity, 1], mres[:]), base + 3)
                V.tensor_tensor(msb[:, parity, 2], mres[:], msb[:, parity, 1], ALU.subtract).then_inc(mt_split, 1)

            def early_tile(i):
                dve.wait_ge(m_full, i + 1)
                V.tensor_reduce(mneg[:, 0, i:i + 1], psE, X_AXIS, ALU.max, negate=True).then_inc(m_free, 1)

            def early(b, c, place):
                for i in early_tiles(b, c, place):
                    early_tile(i)

            def second_parts(b, c, base):
                for t in range(QT):
                    early(b, c, f"v{t}")
                for m in range(DT):
                    early(b, c, f"f{m}")
                    dve.wait_ge(f_taken, 2 + 6 * b + 2 * c + m + 1)
                    chain(V.tensor_tensor(kf[:, m], kf[:, m], parts[:, c, m, 0], ALU.subtract), base + m + 1)
                    V.tensor_copy(parts[:, c, m, 1], kf[:, m]).then_inc(r_ok, 1)

            dve.wait_ge(wA_hi, 1)
            V.tensor_tensor(wAL[:].rearrange("p a k c -> p (a k c)"), wA_raw[:].rearrange("p a k c -> p (a k c)"),
                            wAH[:].bitcast(F32).rearrange("p a k c -> p (a k c)"), ALU.subtract).then_inc(wA_ok, 1)
            low(0, 0)
            low(0, 1)
            dve.wait_ge(x0_in, 16)
            variances(x_rows(0), 0)
            normalise(x_rows(0), zA, z_ok, 1, 2)
            dve.wait_ge(x_in, 16 * (NB - 1))
            A_LINKS = 2 + 5 + 6

            def phase_a(b, last):
                base = b * A_LINKS + 7
                second_parts(b, 0, base)
                low(b, 2)
                if not last:
                    variances(x_rows(b + 1), base + 2)
                    second_parts(b, 1, base + 4)
                    low(b + 1, 0)
                    normalise(x_rows(b + 1), zA, z_ok, b + 2, base + 6)
                    second_parts(b, 2, base + 11)
                    low(b + 1, 1)
                else:
                    second_parts(b, 1, base + 2)
                    split_max(0, 0, base + 4)
                    second_parts(b, 2, base + 7)

            with dve.Fori(0, NB - 2) as b:
                phase_a(b, False)
            phase_a(NB - 2, False)
            phase_a(NB - 1, True)
            A0 = (NB - 1) * A_LINKS + 7 + 9
            dve.wait_ge(consts, 16 * 5)
            chain(V.tensor_copy(gwH[:], gw_raw[:]), A0 + 1)
            V.tensor_tensor(gwL[:], gw_raw[:], gwH[:].bitcast(F32), ALU.subtract).then_inc(gw_ok, 1)

            B0 = A0 + 1

            def reduce_tile(t, parity, i):
                dve.wait_ge(m_full, t + 1)
                V.tensor_reduce(mneg[:, parity, i:i + 1], psM[:, i % 2], X_AXIS, ALU.max,
                                negate=True).then_inc(m_free, 1)

            for i in range(FIRST):
                reduce_tile(TILES + i, 1, i)
            B1 = B0
            U_LINKS = 4

            def unit(b, u, last):
                n = 4 * b + u
                links = B1 + U_LINKS * n
                for k in range(KT):
                    for j, off, i in max_tiles(u, k):
                        if exists(last, u + off):
                            reduce_tile(AHEAD + TILES * n + j, (u + off) % 2, i)
                    if k == 3 and exists(last, u + 1):
                        split_max(n + 1, (u + 1) % 2, links)
                    if last and u == NG - 1 and k in router:
                        f, before = router[k]
                        f(0, links + before)
                dve.wait_ge(ot_full, n + 1)
                dve.wait_ge(o_taken, n + 1)
                o = psO[:, u % 2].rearrange("p (t h v) -> p t h v", t=QT, h=HG)
                used = U_LINKS if exists(last, u + 1) else RL + 1
                chain(V.reciprocal(rden[:], o[:, :, :, DH]), links + used)
                dve.wait_ge(a_st[u % 2], 16 * (2 * b + u // 2 + 1))
                for t in range(QT):
                    ins = V.tensor_tensor(ast[:, u % 2, t].rearrange("p (h d) -> p h d", d=DH), o[:, t, :, 0:DH],
                                          rden[:, t].unsqueeze(2).to_broadcast([P, HG, DH]), ALU.mult)
                    if t == 0:
                        first = ins
                ins.then_inc(o_taken, 1)

            def r_residual(b, base):
                if not isinstance(b, int):
                    dve.wait_ge(out_st, 16 * b)
                dve.wait_ge(wo_full, b + 1)
                V.tensor_tensor(z2[:], psX[:].rearrange("p a (t d) -> p (a t) d", d=D),
                                bo_s[:].unsqueeze(1).to_broadcast([P, QT, D]), ALU.add).then_inc(dchain, 1)
                dve.wait_ge(dchain, base + 1)
                rows = xs[:, bass.ds(b * QT, QT)]
                chain(V.scalar_tensor_tensor(out=rows, in0=z2[:], scalar=tg[:, 0:1], in1=rows, op0=ALU.mult,
                                             op1=ALU.add), base + 2)
                variances(x_rows(b), base + 2)

            def r_norm(b, base):
                normalise(x_rows(b), z2, z2_ok, NB + 1 + b, base)

            def r_low(b, base):
                for k in range(DT):
                    dve.wait_ge(zt_hi, 2 * b + k + 1)
                    V.tensor_tensor(zTL[:, bass.ds(b % 2, 1), k].rearrange("p a c -> p (a c)"), psX[:, k],
                                    zTH[:, bass.ds(b % 2, 1), k].bitcast(F32).rearrange("p a c -> p (a c)"),
                                    ALU.subtract).then_inc(zt_ok, 1)

            def r_shift(b, base):
                dve.wait_ge(lt_full, b + 1)
                lg = psX[:, 1, 0:QT * NR].rearrange("p (t e) -> p t e", e=NR)
                chain(V.tensor_reduce(small[:, 0], lg, X_AXIS, ALU.max, negate=True), base + 1)
                V.tensor_tensor(pt[:, 0], lg, small[:, 0].unsqueeze(2).to_broadcast([P, QT, NR]),
                                ALU.add).then_inc(d_ok, 1)

            def r_choose(b, base):
                dve.wait_ge(ex_ok, b + 1)
                chain(V.tensor_reduce(small[:, 1], pt[:, 1], X_AXIS, ALU.add), base + 1)
                chain(V.reciprocal(small[:, 2], small[:, 1]), base + 2)
                chain(V.tensor_tensor(pt[:, 2], pt[:, 1], small[:, 2].unsqueeze(2).to_broadcast([P, QT, NR]),
                                      ALU.mult), base + 3)
                for t in range(QT):
                    rows = slice(t * NR, (t + 1) * NR)
                    other = pt[:, 2, t].unsqueeze(1).to_broadcast([P, NR, NR])
                    own = pt[:, 2, t].unsqueeze(2).to_broadcast([P, NR, NR])
                    V.tensor_tensor(cmp[:, 0, rows], other, own, ALU.is_gt)
                    last = V.tensor_tensor(cmp[:, 1, rows], other, own, ALU.is_equal)
                chain(last, base + 4)
                for t in range(QT):
                    rows = slice(t * NR, (t + 1) * NR)
                    last = V.tensor_tensor(cmp[:, 1, rows], cmp[:, 1, rows], trimask[:], ALU.mult)
                chain(last, base + 5)
                chain(V.tensor_tensor(cmp[:, 0], cmp[:, 0], cmp[:, 1], ALU.add), base + 6)
                chain(V.tensor_reduce(rank[:], cmp[:, 0], X_AXIS, ALU.add), base + 7)
                V.scalar_tensor_tensor(out=pt[:, 3].rearrange("p t e -> p (t e)"), in0=rank[:], scalar=1.5,
                                       in1=pt[:, 2].rearrange("p t e -> p (t e)"), op0=ALU.is_lt,
                                       op1=ALU.mult).then_inc(cw_ok, 1)

            router = {1: (r_residual, 0), 2: (r_norm, 4), 3: (r_low, 9), 5: (r_shift, 9), 6: (r_choose, 10)}
            RL = 17

            with dve.Fori(0, NB - 1) as b:
                for u in range(NG):
                    unit(b, u, False)
            for u in range(NG):
                if u == NG - 1:
                    dve.wait_ge(c_in, 16 * 4)
                    dve.wait_ge(tanh_ok, 1)
                    dve.wait_ge(cw_ones, 1)
                unit(NB - 1, u, True)
            C1 = B1 + U_LINKS * (UNITS - 1) + RL + 1
            E_LINKS = 2 * NR + RL

            def gate(b, e, j, value):
                dve.wait_ge(sil_ok, 18 * b + 2 * e + j + 1)
                if e:
                    if j == 0:
                        dve.wait_ge(cwb_ld[e % 2], 16 * (4 * b + (e + 1) // 2))
                    chain(V.tensor_tensor(sil[:, j], sil[:, j], cwb[:, e % 2], ALU.mult), value)
                elif not isinstance(b, int):
                    dve.wait_ge(gl_ok, 18 * b - 1 + j)
                V.scalar_tensor_tensor(out=g[:, j], in0=psH[:, j, 1], scalar=b1_s[:, e, 2 + j:3 + j],
                                       in1=sil[:, j], op0=ALU.add, op1=ALU.mult).then_inc(g_ok, 1)

            def gated_low(b, e, j):
                dve.wait_ge(gh_ok, 18 * b + 2 * e + j + 1)
                V.tensor_tensor(gL[:, e % 2, j], g[:, j], gH[:, e % 2, j].bitcast(F32),
                                ALU.subtract).then_inc(gl_ok, 1)

            for s in range(2):
                dve.wait_ge(a_st[s], 16 + 16 * UNITS // 2)
            gate(0, 0, 0, 0)
            gate(0, 0, 1, 0)
            gated_low(0, 0, 0)

            def experts(b, last):
                links = C1 + E_LINKS * b
                count = 0
                for e in range(1, NE):
                    count += 1
                    gate(b, e, 0, links + count)
                    gated_low(b, e - 1, 1)
                    count += 1
                    gate(b, e, 1, links + count)
                    gated_low(b, e, 0)
                    if not last and e - 1 in router:
                        f, before = router[e - 1]
                        f(b + 1, links + count)
                        count += {1: 4, 2: 5, 3: 0, 5: 1, 6: 7}[e - 1]
                gated_low(b, NE - 1, 1)
                if not last:
                    gate(b + 1, 0, 0, 0)
                    gate(b + 1, 0, 1, 0)
                    gated_low(b + 1, 0, 0)
                dve.wait_ge(yt_full, b + 1)
                if last:
                    dve.wait_ge(out_st, 16 * (b + 1))
                V.scalar_tensor_tensor(out=o_s[:], in0=psY[:].rearrange("p a (t d) -> p (a t) d", d=D),
                                       scalar=tg[:, 1:2], in1=xs[:, bass.ds(b * QT, QT)], op0=ALU.mult,
                                       op1=ALU.add).then_inc(y_taken, 1)

            with dve.Fori(0, NB - 1) as b:
                experts(b, False)
            experts(NB - 1, True)

        @block.tensor
        def _(pe):
            mm, tr = nc.tensor.matmul, nc.tensor.transpose

            pe.wait_ge(idn_in, 16)

            def turn(b, c):
                src = zA if c == 2 else ctxt[:, c]
                if c == 2:
                    pe.wait_ge(z_ok, b + 1)
                else:
                    pe.wait_ge(ctx_ld[c], 16 * (b + 1))
                for k in range(DT):
                    pe.wait_ge(t_split, 6 * b + 2 * c + k + 1)
                    for t in range(QT):
                        last = tr(psT[:, k, t * P:(t + 1) * P], src[:, t, k * P:(k + 1) * P], idn[:])
                    last.then_inc(t_full, 1)

            def turn_max(n, parity, tiles, first=False):
                pe.wait_ge(m_free, 2 + tiles)
                if not first:
                    pe.wait_ge(o_taken, n)
                tr(psO[0:TILES, parity, 0:P], mneg[:, parity], idn[:]).then_inc(mt_full, 1)

            def early(b, c, place):
                for i in early_tiles(b, c, place):
                    if i == 0:
                        pe.wait_ge(unit_ld[0], 16 * 12)
                    else:
                        pe.wait_ge(m_free, 2 + i)
                    h, qt = divmod(i, QT)
                    for half in range(2):
                        last = mm(psE[:, half * BLK:(half + 1) * BLK],
                                  qst[0:SROWS, 0, h, qt * P:(qt + 1) * P],
                                  kst[0:SROWS, 0, h, half * BLK:(half + 1) * BLK], start=True, stop=True)
                    last.then_inc(m_full, 1)

            def project(b, c):
                pe.wait_ge(t_split, 2 + 6 * b + 2 * c + 2)
                terms = ((wAH, tH), (wAL, tH), (wAH, tL))
                if c < 2:
                    for t in range(QT):
                        if t % 2 == 0:
                            pe.wait_ge(v_taken, 4 * b + 2 * c + t // 2 + 1)
                        for i, (wt, tt) in enumerate(terms):
                            for k in range(DT):
                                last = mm(psV[:, t // 2, t % 2], tt[:, c, k, t * P:(t + 1) * P], wt[:, 2, k],
                                          start=(i == 0 and k == 0), stop=(i == 2 and k == DT - 1))
                        if t % 2:
                            last.then_inc(v_full, 1)
                        early(b, c, f"v{t}")
                w = 0 if c == 2 else 1
                for m in range(DT):
                    pe.wait_ge(f_taken, 6 * b + 2 * c + m + 1)
                    for i, (wt, tt) in enumerate(terms):
                        for k in range(DT):
                            last = mm(psF[:, m], wt[:, w, k, m * P:(m + 1) * P], tt[:, c, k],
                                      start=(i == 0 and k == 0), stop=(i == 2 and k == DT - 1))
                    last.then_inc(f_full, 1)
                    early(b, c, f"f{m}")
                    if m == 0 and c == 2 and isinstance(b, int) and b == NB - 1:
                        turn_max(0, 0, TILES, first=True)

            def phase_a(b, last):
                project(b, 0)
                turn(b, 2)
                project(b, 1)
                if not last:
                    turn(b + 1, 0)
                project(b, 2)
                if not last:
                    turn(b + 1, 1)

            turn(0, 0)
            turn(0, 1)
            pe.wait_ge(wA_ok, 1)
            with pe.Fori(0, NB - 2) as b:
                phase_a(b, False)
            phase_a(NB - 2, False)
            phase_a(NB - 1, True)

            def max_tile(t, slot, i):
                h, qt = divmod(i, QT)
                pe.wait_ge(m_free, t + 1)
                for half in range(2):
                    last = mm(psM[:, i % 2, half * BLK:(half + 1) * BLK],
                              qst[0:SROWS, slot, h, qt * P:(qt + 1) * P],
                              kst[0:SROWS, slot, h, half * BLK:(half + 1) * BLK], start=True, stop=True)
                last.then_inc(m_full, 1)

            def score_tile(s, slot, kt, j):
                pe.wait_ge(e_done, 4 * s + j + 1)
                mm(psS[:, j % 2], kst[:, slot, j, kt * P:(kt + 1) * P], qst[:, slot, j], start=True,
                   stop=True).then_inc(s_full, 1)

            pe.wait_ge(f_taken, 2 + 6 * NB)
            pe.wait_ge(v_taken, 2 + 4 * NB)
            pe.wait_ge(ones_k, 1)
            pe.wait_ge(unit_ld[1], 16 * 12)
            for i in range(FIRST):
                max_tile(TILES + i, 1, i)
                if i == 3:
                    pe.wait_ge(m_ld[0], 48)
                if i >= 3 and i - 3 < LEAD * HG:
                    step, j = divmod(i - 3, HG)
                    score_tile(step, 0, step, j)
            for i in range(FIRST - 3, LEAD * HG):
                step, j = divmod(i, HG)
                score_tile(step, 0, step, j)

            def values(b, u, k):
                n = 4 * b + u
                if k == 0:
                    pe.wait_ge(mt_split, n + 1)
                    pe.wait_ge(v_ld[u], 16 * (b + 1))
                pe.wait_ge(e_done, 2 + 4 * (8 * n + k + 1))
                for j in range(HG):
                    last = mm(psO[j * VW:(j + 1) * VW, u % 2], vt[:, u, k, j * VW:(j + 1) * VW], pr[:, k % 4, j],
                              start=(k == 0), stop=(k == KT - 1), skip_group_check=True)
                last.then_inc(pv_done, 1)

            def unit(b, u, last):
                n = 4 * b + u
                for k in range(KT):
                    nxt, kt = divmod(k + LEAD, KT)
                    slot = (u + nxt) % NG
                    ahead = exists(last, u + nxt)
                    tiles = [(j, off, i) for j, off, i in max_tiles(u, k) if exists(last, u + off)]
                    if ahead and kt == 0:
                        pe.wait_ge(m_ld[slot], 48 * (b + 1 + (u + 1) // NG))

                    def score(j):
                        if ahead:
                            score_tile(8 * n + k + LEAD, slot, kt, j)

                    score(0)
                    score(1)
                    values(b, u, k)
                    score(2)
                    score(3)
                    for j, off, i in tiles:
                        if off == 2 and i == 0:
                            pe.wait_ge(unit_ld[(u + 2) % NG], 16 * 12 * (b + 1 + (u + 2) // NG))
                        max_tile(AHEAD + TILES * n + j, (u + off) % NG, i)
                    if k == 3 and exists(last, u + 1):
                        turn_max(n + 1, (u + 1) % 2, AHEAD + TILES * n + REST)
                    if last and u == NG - 1 and k in router:
                        router[k](0)
                pe.wait_ge(o_copied, n + 1)
                for t in range(QT):
                    fin = tr(psO[:, u % 2, t * P:(t + 1) * P], osb[:, t * P:(t + 1) * P], idn[:])
                fin.then_inc(ot_full, 1)

            def r_attn(b):
                pe.wait_ge(a_ld, 16 * (b + 1))
                if not isinstance(b, int):
                    pe.wait_ge(cwt_ok, b)
                for k in range(DT):
                    for t in range(QT):
                        last = tr(psX[:, k, t * P:(t + 1) * P], a_in[:, t, k * P:(k + 1) * P], idn[:])
                last.then_inc(at_full, 1)

            def r_wo(b):
                pe.wait_ge(at_ok, 2 * b + 2)
                for t in range(QT):
                    for k in range(DT):
                        last = mm(psX[:, t // 2, (t % 2) * D:(t % 2 + 1) * D], aT[:, k, t * P:(t + 1) * P], wo_s[:, k],
                                  start=(k == 0), stop=(k == DT - 1))
                last.then_inc(wo_full, 1)

            def r_turn(b):
                pe.wait_ge(z2_ok, b + 1)
                for k in range(DT):
                    for t in range(QT):
                        last = tr(psX[:, k, t * P:(t + 1) * P], z2[:, t, k * P:(k + 1) * P], idn[:])
                last.then_inc(zt_full, 1)

            def zt(part, b, k):
                return (zTH, zTL)[part][:, bass.ds(b % 2, 1), k].rearrange("p a c -> p (a c)")

            def r_logits(b):
                pe.wait_ge(zt_ok, 2 * b + 2)
                for i, (wt, part) in enumerate(((gwH, 0), (gwL, 0), (gwH, 1))):
                    for k in range(DT):
                        last = mm(psX[0:NR, 0], wt[:, k], zt(part, b, k), start=(i == 0 and k == 0),
                                  stop=(i == 2 and k == DT - 1))
                last.then_inc(lg_full, 1)

            def r_lturn(b):
                pe.wait_ge(lg_sb, b + 1)
                for t in range(QT):
                    last = mm(psX[:, 1, t * NR:(t + 1) * NR], lT[:, t * P:(t + 1) * P], idn[0:NR, 0:NR],
                              start=True, stop=True)
                last.then_inc(lt_full, 1)

            def r_cturn(b):
                pe.wait_ge(cw_ok, b + 1)
                for t in range(QT):
                    last = tr(psX[0:NR, 0, t * P:(t + 1) * P], pt[:, 3, t], idn[:])
                last.then_inc(cwt_full, 1)

            router = {0: r_attn, 1: r_wo, 3: r_turn, 4: r_logits, 5: r_lturn, 7: r_cturn}

            with pe.Fori(0, NB - 1) as b:
                for u in range(NG):
                    unit(b, u, False)
            for u in range(NG):
                if u == NG - 1:
                    pe.wait_ge(c_in, 16 * 4)
                    pe.wait_ge(gw_ok, 1)
                    pe.wait_ge(m_free, 2 + UNITS * TILES)
                unit(NB - 1, u, True)

            def second(b, e, k, stop=False):
                pe.wait_ge(gl_ok, 18 * b + 2 * e + k + 1)
                if e == 0 and k == 0:
                    pe.wait_ge(y_taken, b + 1)
                for m in range(DT):
                    for i, (part, gt) in enumerate(((0, gH), (1, gH), (0, gL))):
                        last = mm(psY[:, m], w2(e, part)[:, k, m * P:(m + 1) * P], gt[:, e % 2, k],
                                  start=(e == 0 and k == 0 and i == 0), stop=(stop and i == 2))
                if k:
                    last.then_inc(w2_done, 1)

            def first(b, e, j):
                pe.wait_ge(g_ok, 18 * b + 2 * e + j + 1)
                for ab in range(2):
                    m = 2 * ab + j
                    for i, (wp, zp) in enumerate(((0, 0), (1, 0), (0, 1))):
                        for k in range(DT):
                            last = mm(psH[:, j, ab], w1(e, wp)[:, k, m * P:(m + 1) * P], zt(zp, b, k),
                                      start=(i == 0 and k == 0), stop=(i == 2 and k == DT - 1))
                last.then_inc(h_full, 1)

            def turn_sum(b):
                pe.wait_ge(y_copied, 2 * b + 2)
                for t in range(QT):
                    for m in range(DT):
                        last = tr(psY[:, t // 2, (t % 2) * D + m * P:(t % 2) * D + (m + 1) * P],
                                  yT[:, m, t * P:(t + 1) * P], idn[:])
                last.then_inc(yt_full, 1)

            def experts(b, last):
                for e in range(1, NE):
                    pe.wait_ge(w_ok, e + 1)
                    first(b, e, 0)
                    first(b, e, 1)
                    second(b, e - 1, 0)
                    second(b, e - 1, 1)
                    if not last and e - 1 in router:
                        router[e - 1](b + 1)
                if not last:
                    pe.wait_ge(zt_ok, 2 * b + 4)
                    first(b + 1, 0, 0)
                pe.wait_ge(cwt_ok, b + 1)
                for m in range(DT):
                    mm(psY[:, m], b2_s[:, m * P:(m + 1) * P], cw_of(b), start=False, stop=False)
                second(b, NE - 1, 0)
                second(b, NE - 1, 1, stop=True)
                if not last:
                    first(b + 1, 0, 1)
                turn_sum(b)

            pe.wait_ge(w_ok, 1)
            pe.wait_ge(zt_ok, 2)
            first(0, 0, 0)
            first(0, 0, 1)
            pe.wait_ge(o_taken, UNITS + 1)
            with pe.Fori(0, NB - 1) as b:
                experts(b, False)
            experts(NB - 1, True)


def kernel(x, ctx_1024, g_xattn, g_ffn, L0_xattn_Wq, L0_xattn_bq, L0_xattn_Wk, L0_xattn_bk, L0_xattn_Wv,
           L0_xattn_bv, L0_xattn_Wo, L0_xattn_bo, L0_ffn_gate_w, L0_ffn_gate_b, L0_ffn_sw1, L0_ffn_sb1,
           L0_ffn_sw2, L0_ffn_sb2, L0_ffn_rw1, L0_ffn_rb1, L0_ffn_rw2, L0_ffn_rb2):
    import numpy as np
    import concourse.bacc as bacc
    from concourse.bass_utils import run_bass_kernel_spmd

    def rows(w):
        w = np.asarray(w)
        return w.reshape(w.shape[0] // P, P, w.shape[1]).transpose(1, 0, 2)

    def spread(v, n=P):
        return np.broadcast_to(np.asarray(v), (n, np.asarray(v).shape[0]))

    w1 = np.concatenate([np.asarray(L0_ffn_sw1), np.asarray(L0_ffn_rw1)])
    w2 = np.concatenate([np.asarray(L0_ffn_sw2), np.asarray(L0_ffn_rw2)])
    b1 = np.concatenate([np.asarray(L0_ffn_sb1), np.asarray(L0_ffn_rb1)])
    arrays = {
        "x": x, "ctx": ctx_1024,
        "gates": spread(np.concatenate([np.asarray(g_xattn), np.asarray(g_ffn)])),
        "wqkv": np.stack([rows(np.asarray(w).T) for w in (L0_xattn_Wq, L0_xattn_Wk, L0_xattn_Wv)], axis=1),
        "bqkv": np.stack([np.asarray(v).reshape(DT, P).T for v in (L0_xattn_bq, L0_xattn_bk, L0_xattn_bv)], axis=1),
        "wo": rows(np.asarray(L0_xattn_Wo).T), "bo": spread(L0_xattn_bo),
        "gate_w": rows(L0_ffn_gate_w), "gate_b": np.asarray(L0_ffn_gate_b).reshape(NR, 1),
        "wexp": np.stack([np.concatenate([rows(a).reshape(P, -1), rows(c).reshape(P, -1)], axis=1)
                          for a, c in zip(w1, w2)]),
        "b1": b1.reshape(NE, 4, P).transpose(2, 0, 1),
        "b2": np.concatenate([np.asarray(L0_ffn_rb2), np.asarray(L0_ffn_sb2)]),
        "ident": np.eye(P, dtype=np.float32),
        "tri": np.broadcast_to(np.tril(np.ones((NR, NR), np.float32), -1), (P, NR, NR)),
    }
    arrays = {k: np.ascontiguousarray(v) for k, v in arrays.items()}
    nc = bacc.Bacc("TRN2", target_bir_lowering=False, num_devices=1)
    args = [nc.dram_tensor(k, v.shape, mybir.dt.from_np(v.dtype), kind="ExternalInput").ap()
            for k, v in arrays.items()]
    out = nc.dram_tensor("out", (NB, NQ, D), F32, kind="ExternalOutput").ap()
    build(nc, *args, out)
    r = run_bass_kernel_spmd(nc, [arrays], core_ids=[0])
    return r.results[0]["out"]
```

```python
import math
from contextlib import ExitStack

import concourse.bass as bass
from concourse import mybir

F32 = mybir.dt.float32
F32R = mybir.dt.float32r
BF16 = mybir.dt.bfloat16
ALU = mybir.AluOpType
ACT = mybir.ActivationFunctionType
X_AXIS = mybir.AxisListType.X

P = 128
NB, NQ, NK, D = 4, 512, 1024, 256
NH, DH = 16, 16
DT = D // P
QT = NQ // P
KT = NK // P
HG = 4
NG = NH // HG
UNITS = NB * NG
TERMS = ((0, 0), (0, 1), (1, 0), (1, 1), (0, 2), (2, 0))
SROWS = len(TERMS) * DH
MROWS = SROWS + 3
VW = 32
NE = 9
NR = NE - 1
FF = 256
EARLY = 3
WCOLS = DT * 2 * FF + DT * D
BLK = 512
EPS = 1e-5
SCALE = 1.0 / DH ** 0.5


def build(nc, x, ctx_in, gates, wqkv, bqkv, wo, bo, gate_w, gate_b, wexp, b1, b2, ident, tri, out):
    dram = lambda name, shape, dt: nc.dram_tensor(name, shape, dt, kind="Internal").ap()
    q_parts = dram("q_parts", [NB, 3, D, NQ], BF16)
    k_parts = dram("k_parts", [NB, 3, D, NK], BF16)
    v_pad = dram("v_pad", [NB, KT, P, NH * VW], F32)
    attn = dram("attn", [NB, P, QT, D], F32)
    cw_rows = dram("cw_rows", [NR, NB * NQ], F32)

    with ExitStack() as es:
        sb = lambda name, shape, dt=F32, st=es: st.enter_context(nc.sbuf_tensor(name, shape, dt))
        ps = lambda name, shape, st=es: st.enter_context(nc.psum_tensor(name, shape, F32))
        sem = lambda name: es.enter_context(nc.semaphore(name))

        xs = sb("xs", [P, NB * QT, D])
        idn = sb("idn", [P, P])
        eW1H = sb("eW1H", [P, EARLY, DT, 2 * FF], F32R)
        eW1L = sb("eW1L", [P, EARLY, DT, 2 * FF], F32R)
        eW2H = sb("eW2H", [P, EARLY, DT, D], F32R)
        eW2L = sb("eW2L", [P, EARLY, DT, D], F32R)
        wraw = sb("wraw", [P, 2, WCOLS])
        trimask = sb("trimask", [P, NR, NR])
        tg_in = sb("tg_in", [P, 2])
        tg = sb("tg", [P, 2])
        bq_s = sb("bq_s", [P, 3, DT])
        gb_s = sb("gb_s", [NR, 1])
        gw_raw = sb("gw_raw", [P, DT, NR])
        gwH = sb("gwH", [P, DT, NR], F32R)
        gwL = sb("gwL", [P, DT, NR], F32R)
        blank = sb("blank", [P, 1])
        warm = sb("warm", [P, 1])
        none = sb("none", [HG * QT, 1])
        stats = sb("stats", [P, QT, 6])
        mv = sb("mv", [P, QT, 2])
        veps = sb("veps", [P, QT])
        std = sb("std", [P, QT])
        rstd = sb("rstd", [P, QT])
        nt = sb("nt", [P, QT])

        sa = ExitStack()
        a_names = [("parts", [P, 3, DT, 3, BLK], BF16), ("vst", [P, 4, 2, NH, VW], F32), ("kf", [P, 2, BLK], F32),
                   ("wA_raw", [P, 3, DT, D], F32), ("ctxt", [P, 2, DT, BLK], F32), ("zA", [P, QT, D], F32),
                   ("wAH", [P, 3, DT, D], F32R), ("wAL", [P, 3, DT, D], F32R), ("tH", [P, 3, DT, BLK], F32R),
                   ("tL", [P, 3, DT, BLK], F32R)]
        parts, vst, kf, wA_raw, ctxt, zA, wAH, wAL, tH, tL = (sb(*a, sa) for a in a_names)
        sa.close()
        nbytes = lambda shape, dt: (2 if dt == BF16 else 4) * math.prod(shape[1:])
        z_names = [("zTH", [P, 2, DT, BLK], F32R), ("zTL", [P, 2, DT, BLK], F32R), ("a_in", [P, QT, D], F32),
                   ("aT", [P, DT, BLK], F32), ("wo_s", [P, DT, D], F32), ("bo_s", [P, D], F32),
                   ("z2", [P, QT, D], F32), ("pt", [P, 4, QT, NR], F32), ("small", [P, 3, QT], F32),
                   ("cmp", [P, 2, QT * NR, NR], F32), ("rank", [P, QT * NR], F32), ("cwT", [NE, 2, BLK], F32),
                   ("b1_s", [P, NE, 4], F32), ("b2_s", [NE, D], F32)]
        zTH, zTL, a_in, aT, wo_s, bo_s, z2, pt, small, cmp, rank, cwT, b1_s, b2_s = (sb(*a) for a in z_names)
        lT = cmp[0:NR].rearrange("e a r n -> e (a r n)")
        sB = ExitStack()
        b_names = [("pr", [P, 4, HG, NQ], F32), ("vt", [P, NG, KT, HG * VW], F32), ("osb", [P, NQ], F32),
                   ("rden", [P, QT * HG], F32), ("ast", [P, 2, QT, HG * DH], F32)]
        pr, vt, osb, rden, ast = (sb(*b, sB) for b in b_names)
        over = sum(nbytes(a, t) for _, a, t in a_names) - sum(nbytes(a, t) for _, a, t in z_names + b_names)
        if over > -64:
            sb("gap", [P, over // 4 + 32], F32, sB)
        mneg = sb("mneg", [P, 2, HG * QT], F32, sB)
        msb = sb("msb", [HG * QT, 2, 3, P], BF16, sB)
        mcp = sb("mcp", [HG * QT, P], F32, sB)
        kst = sb("kst", [MROWS, NG, HG, NK], BF16, sB)
        qst = sb("qst", [MROWS, NG, HG, NQ], BF16, sB)
        sB.close()
        lW1H = sb("lW1H", [P, NE - EARLY, DT, 2 * FF], F32R)
        lW1L = sb("lW1L", [P, NE - EARLY, DT, 2 * FF], F32R)
        lW2H = sb("lW2H", [P, NE - EARLY, DT, D], F32R)
        lW2L = sb("lW2L", [P, NE - EARLY, DT, D], F32R)
        cwb = sb("cwb", [P, 2, BLK])
        sil = sb("sil", [P, 2, BLK])
        g = sb("g", [P, 2, BLK])
        gH = sb("gH", [P, 2, 2, BLK], F32R)
        gL = sb("gL", [P, 2, 2, BLK], F32R)
        yT = aT
        o_s = z2

        pa = ExitStack()
        psT = ps("psT", [P, DT, BLK], pa)
        psF = ps("psF", [P, DT, BLK], pa)
        psV = ps("psV", [P, 2, 2, D], pa)
        pa.close()
        pb = ExitStack()
        psM = ps("psM", [P, 2, NK], pb)
        psS = ps("psS", [P, 2, NQ], pb)
        psO = ps("psO", [P, 2, NQ], pb)
        pb.close()
        psX = ps("psX", [P, 2, BLK])
        psH = ps("psH", [P, 2, 2, BLK])
        psY = ps("psY", [P, 2, BLK])
        psE = psO[:].rearrange("p a t -> p (a t)")

        consts = sem("consts"); idn_in = sem("idn_in")
        wkv_in = sem("wkv_in"); wq_in = sem("wq_in")
        x0_in = sem("x0_in"); x_in = sem("x_in")
        ctx_ld = [sem("ctx_in0"), sem("ctx_in1")]
        c_in = sem("c_in"); v_ld = [sem(f"unit_v_in{s}") for s in range(NG)]
        wA_hi = sem("wA_hi"); wA_ok = sem("wA_ok")
        gw_ok = sem("gw_ok")
        dchain = sem("dve_chain")
        tanh_ok = sem("tanh_ok")
        var_ok = sem("var_ok"); std_ok = sem("std_ok"); z_ok = sem("z_ok")
        t_full = sem("t_full"); t_hi = sem("t_hi"); t_split = sem("t_split")
        f_full = sem("f_full"); f_taken = sem("f_taken"); r_ok = sem("r_ok"); k_ok = sem("k_parts_ok")
        v_full = sem("v_full"); v_taken = sem("v_taken")
        qk_st = [sem(f"parts_stored{c}") for c in range(3)]
        v_st = [sem(f"v_stored{s}") for s in range(4)]
        pads = sem("pads"); ones_k = sem("ones_k"); cw_ones = sem("cw_ones")
        unit_ld = [sem(f"unit_in{s}") for s in range(NG)]
        m_ld = [sem(f"max_in{s}") for s in range(NG)]
        m_full = sem("m_full"); m_free = sem("m_free")
        mt_full = sem("mt_full"); mt_copied = sem("mt_copied"); mt_split = sem("mt_split"); m_chain = sem("m_chain"); none_ok = sem("none_ok")
        s_full = sem("s_full"); e_done = sem("exp_done")
        pv_done = sem("pv_done")
        o_copied = sem("o_copied"); ot_full = sem("ot_full"); o_taken = sem("o_taken")
        a_st = [sem("a_stored0"), sem("a_stored1")]
        raw_ld = [sem("raw_in0"), sem("raw_in1")]
        pool_c = sem("pool_chain"); w_ok = sem("w_ok")
        a_ld = sem("a_in"); at_full = sem("at_full"); at_ok = sem("at_ok")
        wo_full = sem("wo_full"); z2_ok = sem("z2_ok"); zt_full = sem("zt_full")
        zt_hi = sem("zt_hi"); zt_ok = sem("zt_ok")
        lg_full = sem("lg_full"); lg_sb = sem("lg_sb"); lt_full = sem("lt_full")
        d_ok = sem("d_ok"); ex_ok = sem("ex_ok"); cw_ok = sem("cw_ok")
        cwt_full = sem("cwt_full"); cwt_ok = sem("cwt_ok"); cw_st = sem("cw_stored")
        cwb_ld = [sem("cwb_in0"), sem("cwb_in1")]
        h_full = sem("h_full"); sil_ok = sem("sil_ok"); g_ok = sem("g_ok")
        gh_ok = sem("gh_ok"); gl_ok = sem("gl_ok"); w2_done = sem("w2_done")
        y_copied = sem("y_copied"); yt_full = sem("yt_full")
        y_taken = sem("y_taken"); out_st = sem("out_stored")

        def w1(e, part):
            return (eW1H, eW1L)[part][:, e] if e < EARLY else (lW1H, lW1L)[part][:, e - EARLY]

        def w2(e, part):
            return (eW2H, eW2L)[part][:, e] if e < EARLY else (lW2H, lW2L)[part][:, e - EARLY]

        def cw_of(b):
            return cwT[:, bass.ds(b % 2, 1)].rearrange("e a t -> e (a t)")

        TILES = HG * QT
        FIRST = 12
        REST = TILES - FIRST
        AHEAD = TILES + FIRST
        MAX_TURN = 2
        MAX_COPY = 3
        LEAD = 2

        EARLY_PLACES = [(NB - 2, 1, place) for place in ("v1", "v3", "f0", "f1")]
        EARLY_PLACES += [(NB - 2, 2, place) for place in ("f0", "f1")]
        EARLY_PLACES += [(NB - 1, c, place) for c in range(2) for place in ("v1", "v2", "v3", "f0", "f1")]

        def early_tiles(b, c, place):
            if not isinstance(b, int):
                return []
            return [i for i, where in enumerate(EARLY_PLACES) if where == (b, c, place)]

        TAIL = KT * (UNITS - 2) + 2 + LEAD
        ROUTER_AT = KT * (NG - 2) + 3

        def score_bank(s, j):
            if isinstance(s, int) and s >= TAIL and j >= 2:
                return psM[:, 1, (j - 2) * NQ:(j - 1) * NQ]
            return psS[:, j % 2]

        def router_stage(u, k, last):
            stage = KT * u + k - ROUTER_AT
            return stage if last and stage >= 0 else None

        def max_tiles(u, step):
            for j in (2 * step, 2 * step + 1):
                yield (j, 1, FIRST + j) if j < REST else (j, 2, j - REST)

        def exists(last, u):
            return not last or u < NG

        block = es.enter_context(nc.Block())

        @block.sync
        def _(sp):
            sp.dma_start(ctxt[:, 0], ctx_in[0, :, 0:BLK].rearrange("(k p) t -> p k t", p=P)).then_inc(ctx_ld[0], 16)
            sp.dma_start(idn[:], ident).then_inc(idn_in, 16)
            sp.dma_start(wA_raw[:, 1:3], wqkv[:, 1:3]).then_inc(wkv_in, 16)
            sp.dma_start(ctxt[:, 1], ctx_in[0, :, BLK:2 * BLK].rearrange("(k p) t -> p k t", p=P)).then_inc(ctx_ld[1], 16)
            sp.dma_start(wA_raw[:, 0], wqkv[:, 0]).then_inc(wq_in, 16)
            sp.dma_start(xs[:, 0:QT, :], x[0].rearrange("(t p) d -> p t d", p=P)).then_inc(x0_in, 16)
            sp.dma_start(tg_in[:], gates).then_inc(consts, 16)
            sp.dma_start(bq_s[:], bqkv).then_inc(consts, 16)
            sp.dma_start(gw_raw[:], gate_w).then_inc(consts, 16)
            sp.dma_start(gb_s[:], gate_b).then_inc(consts, 16)
            sp.dma_start(trimask[:], tri).then_inc(consts, 16)
            for b in range(1, NB):
                sp.dma_start(xs[:, b * QT:(b + 1) * QT, :],
                             x[b].rearrange("(t p) d -> p t d", p=P)).then_inc(x_in, 16)

            def stores(b, load_next, beside=None):
                if load_next:
                    for h in range(2):
                        sp.wait_ge(t_split, 6 * b + 2 * h + 2)
                        sp.dma_start(ctxt[:, h], ctx_in[b + 1, :, h * BLK:(h + 1) * BLK].rearrange(
                            "(k p) t -> p k t", p=P)).then_inc(ctx_ld[h], 16)
                for c in range(3):
                    if c == 1 and beside:
                        beside()
                    if c < 2:
                        for s in range(2):
                            slot = 2 * c + s
                            sp.wait_ge(v_taken, 2 + 4 * b + slot + 1)
                            sp.dma_start(v_pad[b, 2 * slot:2 * slot + 2].rearrange("t p c -> p t c"),
                                         vst[:, slot].rearrange("p t h v -> p t (h v)")).then_inc(v_st[slot], 16)
                    for m in range(DT):
                        sp.wait_ge(k_ok, 2 + 6 * b + 2 * c + m + 1)
                        dst = q_parts[b] if c == 2 else k_parts[b, :, :, c * BLK:(c + 1) * BLK]
                        sp.dma_start(dst[:, m * P:(m + 1) * P, :].rearrange("s p t -> p s t"),
                                     parts[:, c, m]).then_inc(qk_st[c], 16)

            def load_unit(b, u):
                for t, (qp, kp) in enumerate(TERMS):
                    rows = slice(t * DH, (t + 1) * DH)
                    heads = slice(u * HG * DH, (u + 1) * HG * DH)
                    sp.dma_start(qst[rows, u], q_parts[b, qp, heads, :].rearrange("(h d) t -> d h t", d=DH)
                                 ).then_inc(unit_ld[u], 16)
                    sp.dma_start(kst[rows, u], k_parts[b, kp, heads, :].rearrange("(h d) t -> d h t", d=DH)
                                 ).then_inc(unit_ld[u], 16)

            def load_values(b, u):
                sp.dma_start(vt[:, u], v_pad[b, :, :, u * HG * VW:(u + 1) * HG * VW].rearrange("k p c -> p k c")
                             ).then_inc(v_ld[u], 16)

            def load_max(b, u):
                for s in range(3):
                    sp.dma_start(qst[SROWS + s:SROWS + s + 1, u], msb[:, u % 2, s, :]).then_inc(m_ld[u], 16)

            def first_unit():
                for c in range(3):
                    sp.wait_ge(qk_st[c], 32 + 32)
                load_unit(0, 0)

            stores(0, True)
            stores(1, True, first_unit)
            for b in range(2, NB - 1):
                stores(b, True)
            load_unit(0, 1)

            def first_max():
                sp.wait_ge(mt_split, 1)
                load_max(0, 0)

            stores(NB - 1, False)
            first_max()
            sp.wait_ge(f_full, 6 + 6 * NB)
            for s in range(4):
                sp.wait_ge(v_st[s], 16 + 16)
            load_values(0, 0)
            load_values(0, 1)
            load_unit(0, 2)
            load_values(0, 2)
            load_unit(0, 3)
            load_values(0, 3)
            for c in range(3):
                sp.wait_ge(qk_st[c], 32 + 32 * NB)
            for s in range(4):
                sp.wait_ge(v_st[s], 16 + 16 * NB)

            def unit_dmas(b, u, last):
                if exists(last, u + 1):
                    sp.wait_ge(mt_split, 4 * b + u + 2)
                    load_max(b, (u + 1) % NG)
                if not last:
                    sp.wait_ge(pv_done, 4 + KT * (4 * b + u + 1))
                    load_unit(b + 1, u)
                    load_values(b + 1, u)
                sp.wait_ge(o_taken, 4 * b + u + 2)
                sp.dma_start(attn[b, :, :, u * HG * DH:(u + 1) * HG * DH], ast[:, u % 2]).then_inc(a_st[u % 2], 16)

            with sp.Fori(0, NB - 1) as b:
                for u in range(NG):
                    unit_dmas(b, u, False)
            for s in range(2):
                sp.wait_ge(a_st[s], 16 + 16 * (UNITS - NG) // 2)
            sp.dma_start(a_in[:], attn[0]).then_inc(a_ld, 16)
            sp.dma_start(wo_s[:], wo).then_inc(c_in, 16)
            sp.dma_start(bo_s[:], bo).then_inc(c_in, 16)
            sp.dma_start(b1_s[:], b1).then_inc(c_in, 16)
            sp.dma_start(b2_s[:], b2).then_inc(c_in, 16)
            for u in range(NG):
                unit_dmas(NB - 1, u, True)
            for s in range(2):
                sp.wait_ge(a_st[s], 16 + 16 * UNITS // 2)

            def store_weights(b):
                sp.wait_ge(cwt_ok, b + 1)
                cols = bass.ds(b * BLK, BLK)
                sp.dma_start(cw_rows[:, cols], cw_of(b)[0:NR]).then_inc(cw_st, 16)

            def broadcast_weights(b, e):
                sp.wait_ge(g_ok, 2 + 18 * b + (2 * (e - 1) if e > 2 else 0))
                row = cw_rows[e - 1:e, bass.ds(b * BLK, BLK)]
                sp.dma_start(cwb[:, e % 2, :], row.to_broadcast([P, BLK])).then_inc(cwb_ld[e % 2], 16)

            def expert_dmas(b, last):
                for e in range(3, NE):
                    broadcast_weights(b, e)
                if not last:
                    sp.wait_ge(at_full, b + 2)
                    sp.dma_start(a_in[:], attn[(b + 2) % NB]).then_inc(a_ld, 16)
                    store_weights(b + 1)
                    sp.wait_ge(cw_st, 16 * (b + 2))
                    for e in (1, 2):
                        broadcast_weights(b + 1, e)
                sp.wait_ge(y_taken, b + 2)
                sp.dma_start(out[b].rearrange("(t p) d -> p t d", p=P), o_s[:]).then_inc(out_st, 16)

            sp.wait_ge(at_full, 1)
            sp.dma_start(a_in[:], attn[1]).then_inc(a_ld, 16)
            store_weights(0)
            sp.wait_ge(ot_full, UNITS)
            sp.wait_ge(cw_st, 16)
            for e in (1, 2):
                broadcast_weights(0, e)
            with sp.Fori(0, NB - 1) as b:
                expert_dmas(b, False)
            expert_dmas(NB - 1, True)
            sp.wait_ge(out_st, 16 + 16 * NB)
            sp.wait_ge(a_ld, 16 * (NB + 1))

        @block.gpsimd
        def _(pool):
            for s, n in ((f_full, 6), (f_taken, 2), (k_ok, 2), (v_taken, 2), (m_free, 2), (e_done, 2),
                         (pv_done, 4), (o_taken, 1), (g_ok, 2), (w2_done, 2), (y_taken, 1), (out_st, 16)):
                pool.sem_inc(s, n)
            for c in range(3):
                pool.sem_inc(qk_st[c], 32)
            for s in range(4):
                pool.sem_inc(v_st[s], 16)
            for s in range(2):
                pool.sem_inc(a_st[s], 16)
            nc.gpsimd.memset(none[:], 0.0).then_inc(none_ok, 1)
            pool.wait_ge(none_ok, 1)
            nc.gpsimd.memset(vst[:, :, :, :, DH:VW].rearrange("p a b h v -> p (a b h) v"), 0.0).then_inc(pool_c, 1)
            pool.wait_ge(pool_c, 1)
            nc.gpsimd.memset(vst[:, :, :, :, DH:DH + 1].rearrange("p a b h v -> p (a b h) v"), 1.0).then_inc(pads, 1)
            pool.wait_ge(pads, 1)
            nc.gpsimd.memset(kst[SROWS:MROWS], 1.0).then_inc(ones_k, 1)
            pool.wait_ge(ones_k, 1)


            def split_max(n, parity):
                pool.wait_ge(mt_copied, n + 1)
                nc.gpsimd.tensor_tensor(msb[:, parity, 0], mcp[:], none[:].to_broadcast([HG * QT, P]), ALU.subtract).then_inc(m_chain, 1)
                pool.wait_ge(m_chain, 3 * n + 1)
                nc.gpsimd.tensor_tensor(mcp[:], mcp[:], msb[:, parity, 0], ALU.subtract).then_inc(m_chain, 1)
                pool.wait_ge(m_chain, 3 * n + 2)
                nc.gpsimd.tensor_tensor(msb[:, parity, 1], mcp[:], none[:].to_broadcast([HG * QT, P]), ALU.subtract).then_inc(m_chain, 1)
                pool.wait_ge(m_chain, 3 * n + 3)
                nc.gpsimd.tensor_tensor(msb[:, parity, 2], mcp[:], msb[:, parity, 1], ALU.subtract
                                        ).then_inc(mt_split, 1)

            def third_parts(b):
                for c in range(3):
                    for m in range(DT):
                        pool.wait_ge(r_ok, 6 * b + 2 * c + m + 1)
                        nc.gpsimd.tensor_tensor(parts[:, c, m, 2], kf[:, m], parts[:, c, m, 1],
                                                ALU.subtract).then_inc(k_ok, 1)

            pool.wait_ge(z_ok, 1)
            nc.gpsimd.dma_start(wraw[:, 0], wexp[0]).then_inc(raw_ld[0], 16)
            nc.gpsimd.dma_start(wraw[:, 1], wexp[1]).then_inc(raw_ld[1], 16)
            with pool.Fori(0, NB) as b:
                third_parts(b)
            split_max(0, 0)

            for c in range(3):
                pool.wait_ge(qk_st[c], 32 + 32 * NB)
            for s in range(4):
                pool.wait_ge(v_st[s], 16 + 16 * NB)
            pool.wait_ge(f_full, 6 + 6 * NB)
            nc.gpsimd.memset(cwT[:], 1.0).then_inc(cw_ones, 1)
            pool.wait_ge(cw_ones, 1)

            def prepare(e, r, outs):
                nw1 = DT * 2 * FF
                base = 1 + 3 * e
                hi1, lo1, hi2, lo2 = outs
                raw1, raw2 = wraw[:, r, 0:nw1], wraw[:, r, nw1:WCOLS]
                nc.gpsimd.tensor_copy(hi1, raw1).then_inc(pool_c, 1)
                pool.wait_ge(pool_c, base + 1)
                nc.gpsimd.tensor_tensor(lo1, raw1, hi1.bitcast(F32), ALU.subtract).then_inc(pool_c, 1)
                nc.gpsimd.tensor_copy(hi2, raw2).then_inc(pool_c, 1)
                pool.wait_ge(pool_c, base + 3)
                nc.gpsimd.tensor_tensor(lo2, raw2, hi2.bitcast(F32), ALU.subtract).then_inc(w_ok, 1)
                pool.wait_ge(w_ok, e + 1)

            def flat(tensors, e):
                return tuple(t[:, bass.ds(e, 1)].rearrange("p a k c -> p (a k c)") for t in tensors)

            for u in range(NG):
                split_max(u + 1, (u + 1) % 2)
                if u < EARLY:
                    r = u % 2
                    pool.wait_ge(raw_ld[r], 16 * (u // 2 + 1))
                    prepare(u, r, flat((eW1H, eW1L, eW2H, eW2L), u))
                    nc.gpsimd.dma_start(wraw[:, r], wexp[u + 2]).then_inc(raw_ld[r], 16)
            with pool.Fori(1, NB - 1) as b:
                for u in range(NG):
                    split_max(4 * b + u + 1, (u + 1) % 2)
            for u in range(NG - 1):
                split_max(4 * (NB - 1) + u + 1, (u + 1) % 2)
            pool.wait_ge(ot_full, UNITS)
            for s in range(2):
                pool.wait_ge(a_st[s], 16 + 16 * UNITS // 2)
            for e in range(EARLY, NE):
                r = e % 2
                pool.wait_ge(raw_ld[r], 16 * (e // 2 + 1))
                prepare(e, r, flat((lW1H, lW1L, lW2H, lW2L), e - EARLY))
                if e + 2 < NE:
                    nc.gpsimd.dma_start(wraw[:, r], wexp[e + 2]).then_inc(raw_ld[r], 16)

        @block.scalar
        def _(act):
            def sqrt_of(n):
                act.wait_ge(var_ok, n)
                nc.scalar.activation(std[:], veps[:], ACT.Sqrt).then_inc(std_ok, 1)

            def weights_high(part):
                nc.scalar.copy(wAH[:, part].rearrange("p a k c -> p (a k c)"),
                               wA_raw[:, part].rearrange("p a k c -> p (a k c)")).then_inc(wA_hi, 1)

            act.wait_ge(wkv_in, 16)
            weights_high(slice(1, 3))

            def high(b, c):
                act.wait_ge(f_full, 6 * b + 2 * c + 2)
                if c < 2:
                    act.wait_ge(ctx_ld[c], 16 * (b + 1))
                for k in range(DT):
                    if c == 2:
                        act.wait_ge(t_full, 2 * b + k + 1)
                    nc.scalar.copy(tH[:, c, k], psT[:, k] if c == 2 else ctxt[:, c, k]).then_inc(t_hi, 1)

            def biased(b, c):
                for m in range(DT):
                    i = 6 * b + 2 * c + m
                    act.wait_ge(f_full, 6 + i + 1)
                    act.wait_ge(k_ok, i + 1)
                    act.wait_ge(qk_st[c], 32 * (b + 1))
                    bias = bq_s[:, 0 if c == 2 else 1, m:m + 1]
                    nc.scalar.activation(kf[:, m], psF[:, m], ACT.Identity, bias=bias)
                    nc.scalar.activation(parts[:, c, m, 0], psF[:, m], ACT.Identity,
                                         bias=bias).then_inc(f_taken, 1)

            def values(b, c):
                for s in range(2):
                    slot = 2 * c + s
                    act.wait_ge(v_full, 4 * b + slot + 1)
                    act.wait_ge(v_st[slot], 16 * (b + 1))
                    nc.scalar.copy(vst[:, slot, :, :, 0:DH], psV[:, s].rearrange("p t (h d) -> p t h d", d=DH)
                                   ).then_inc(v_taken, 1)

            def phase_a(b, last):
                values(b, 0)
                biased(b, 0)
                high(b, 2)
                values(b, 1)
                biased(b, 1)
                if not last:
                    high(b + 1, 0)
                    sqrt_of(b + 2)
                biased(b, 2)
                if not last:
                    high(b + 1, 1)

            def copy_max(n, parity):
                act.wait_ge(mt_full, n + 1)
                nc.scalar.copy(mcp[:], psO[0:TILES, parity, 0:P]).then_inc(mt_copied, 1)

            high(0, 0)
            high(0, 1)
            act.wait_ge(wq_in, 16)
            weights_high(slice(0, 1))
            sqrt_of(1)
            act.wait_ge(consts, 16 * 5)
            act.wait_ge(consts, 16 * 5)
            act.wait_ge(pads, 1)
            with act.Fori(0, NB - 1) as b:
                phase_a(b, False)
            phase_a(NB - 1, True)
            copy_max(0, 0)

            nc.scalar.activation(tg[:], tg_in[:], ACT.Tanh).then_inc(tanh_ok, 1)

            def exponentials(s, slot, j):
                if j == 0:
                    act.wait_ge(pv_done, s + 1)
                act.wait_ge(s_full, 4 * s + j + 1)
                nc.scalar.activation(pr[:, slot, j], score_bank(s, j), ACT.Exp, scale=SCALE).then_inc(e_done, 1)

            for s in range(LEAD):
                for j in range(HG):
                    exponentials(s, s % 4, j)

            def unit_exps(b, u, last):
                n = 4 * b + u
                for k in range(KT):
                    ahead = exists(last, u + (k + LEAD) // KT)
                    for j in range(HG):
                        if ahead:
                            exponentials(8 * n + k + LEAD, (k + LEAD) % 4, j)
                        if k == MAX_COPY and j == 0 and exists(last, u + 1):
                            act.wait_ge(mt_split, n + 1)
                            copy_max(n + 1, (u + 1) % 2)
                        if k == KT - 1 and j == 1:
                            act.wait_ge(pv_done, 4 + KT * (n + 1))
                            nc.scalar.copy(osb[:], psO[:, u % 2]).then_inc(o_copied, 1)
                    stage = router_stage(u, k, last)
                    if stage == 0:
                        act.wait_ge(c_in, 16 * 4)
                        act.wait_ge(cw_ones, 1)
                    if stage in beside_attention:
                        beside_attention[stage](0)

            def r_attn(b):
                act.wait_ge(at_full, b + 1)
                for k in range(DT):
                    nc.scalar.activation(aT[:, k], psX[:, k], ACT.Identity,
                                         bias=bq_s[:, 2, k:k + 1]).then_inc(at_ok, 1)

            def r_sqrt(b):
                sqrt_of(NB + 1 + b)

            def r_high(b):
                act.wait_ge(zt_full, b + 1)
                for k in range(DT):
                    nc.scalar.copy(zTH[:, bass.ds(b % 2, 1), k].rearrange("p a c -> p (a c)"), psX[:, k]).then_inc(zt_hi, 1)

            def r_logits(b):
                act.wait_ge(lg_full, b + 1)
                nc.scalar.activation(lT[:], psX[0:NR, 0], ACT.Identity, bias=gb_s[:, 0:1]).then_inc(lg_sb, 1)

            def r_exp(b):
                act.wait_ge(d_ok, b + 1)
                nc.scalar.activation(pt[:, 1], pt[:, 0], ACT.Exp).then_inc(ex_ok, 1)

            def r_cwt(b):
                act.wait_ge(cwt_full, b + 1)
                nc.scalar.copy(cw_of(b)[0:NR], psX[0:NR, 0]).then_inc(cwt_ok, 1)

            router = {0: r_attn, 2: r_sqrt, 3: r_high, 4: r_logits, 5: r_exp, 7: r_cwt}
            beside_attention = {0: r_attn, 4: r_sqrt, 6: r_high, 7: r_logits, 9: r_exp, 12: r_cwt}

            with act.Fori(0, NB - 1) as b:
                for u in range(NG):
                    unit_exps(b, u, False)
            for u in range(NG):
                unit_exps(NB - 1, u, True)

            def silu(b, e, j):
                act.wait_ge(h_full, 18 * b + 2 * e + j + 1)
                nc.scalar.activation(sil[:, j], psH[:, j, 0], ACT.Silu, bias=b1_s[:, e, j:j + 1]).then_inc(sil_ok, 1)

            def gated_high(b, e, j):
                if j == 0:
                    act.wait_ge(w2_done, 9 * b + (e + 1 if e else 2))
                act.wait_ge(g_ok, 2 + 18 * b + 2 * e + j + 1)
                nc.scalar.copy(gH[:, e % 2, j], g[:, j]).then_inc(gh_ok, 1)

            def sum_copy(b):
                act.wait_ge(w2_done, 2 + 9 * (b + 1))
                for m in range(DT):
                    nc.scalar.copy(yT[:, m], psY[:, m]).then_inc(y_copied, 1)

            nc.scalar.activation(warm[:], tg_in[:, 1:2], ACT.Silu)
            for s in range(2):
                act.wait_ge(a_st[s], 16 + 16 * UNITS // 2)
            for j in range(2):
                silu(0, 0, j)
                gated_high(0, 0, j)

            def experts(b, last):
                for e in range(1, NE):
                    for j in range(2):
                        silu(b, e, j)
                        gated_high(b, e, j)
                    if not last and e - 1 in router:
                        router[e - 1](b + 1)
                if not last:
                    silu(b + 1, 0, 0)
                sum_copy(b)
                if not last:
                    gated_high(b + 1, 0, 0)
                    silu(b + 1, 0, 1)
                    gated_high(b + 1, 0, 1)

            with act.Fori(0, NB - 1) as b:
                experts(b, False)
            experts(NB - 1, True)

        @block.vector
        def _(dve):
            V = nc.vector
            def chain(ins, value):
                ins.then_inc(dchain, 1)
                dve.wait_ge(dchain, value)

            NORM1, NORM2 = 3, 7

            def variances(rows, base):
                V.memset(blank[:], 0.0)
                for t in range(QT):
                    last = V.bn_stats(stats[:, t], rows(t))
                chain(last, base + 1)
                V.memset(blank[:], 0.0)
                for t in range(QT):
                    last = V.bn_aggr(mv[:, t], stats[:, t])
                chain(last, base + 2)
                V.tensor_scalar(veps[:], mv[:, :, 1], EPS, None, ALU.add).then_inc(var_ok, 1)

            def normalise(rows, dst, done, nth, base):
                dve.wait_ge(std_ok, nth)
                chain(V.reciprocal(rstd[:], std[:]), base + 1)
                chain(V.tensor_tensor(nt[:], rstd[:], rstd[:], ALU.mult), base + 2)
                chain(V.tensor_tensor(nt[:], nt[:], veps[:], ALU.mult), base + 3)
                chain(V.tensor_scalar(nt[:], nt[:], -0.5, 1.5, ALU.mult, ALU.add), base + 4)
                chain(V.tensor_tensor(rstd[:], rstd[:], nt[:], ALU.mult), base + 5)
                for t in range(QT):
                    last = V.tensor_scalar(dst[:, t], rows(t), mv[:, t, 0:1], rstd[:, t:t + 1],
                                           ALU.subtract, ALU.mult)
                last.then_inc(done, 1)

            def x_rows(b):
                return lambda t: xs[:, bass.ds(b * QT + t, 1)].rearrange("p a d -> p (a d)")

            def low(b, c):
                for k in range(DT):
                    dve.wait_ge(t_hi, 6 * b + 2 * c + k + 1)
                    V.tensor_tensor(tL[:, c, k], psT[:, k] if c == 2 else ctxt[:, c, k], tH[:, c, k].bitcast(F32),
                                    ALU.subtract).then_inc(t_split, 1)

            def early_tile(i):
                dve.wait_ge(m_full, i + 1)
                V.tensor_reduce(mneg[:, 0, i:i + 1], psE, X_AXIS, ALU.max, negate=True).then_inc(m_free, 1)

            def early(b, c, place):
                for i in early_tiles(b, c, place):
                    early_tile(i)

            def early_values(b, c):
                for t in range(QT):
                    early(b, c, f"v{t}")

            def second_parts(b, c, base):
                if c != 1:
                    early_values(b, c)
                for m in range(DT):
                    early(b, c, f"f{m}")
                    dve.wait_ge(f_taken, 2 + 6 * b + 2 * c + m + 1)
                    chain(V.tensor_tensor(kf[:, m], kf[:, m], parts[:, c, m, 0], ALU.subtract), base + m + 1)
                    V.tensor_copy(parts[:, c, m, 1], kf[:, m]).then_inc(r_ok, 1)

            def weights_low(nth, part):
                dve.wait_ge(wA_hi, nth)
                V.tensor_tensor(wAL[:, part].rearrange("p a k c -> p (a k c)"),
                                wA_raw[:, part].rearrange("p a k c -> p (a k c)"),
                                wAH[:, part].bitcast(F32).rearrange("p a k c -> p (a k c)"),
                                ALU.subtract).then_inc(wA_ok, 1)

            weights_low(1, slice(1, 3))
            low(0, 0)
            low(0, 1)
            weights_low(2, slice(0, 1))
            dve.wait_ge(x0_in, 16)
            variances(x_rows(0), 0)
            normalise(x_rows(0), zA, z_ok, 1, 2)
            A_LINKS = 2 + 5 + 6

            def phase_a(b, last):
                base = b * A_LINKS + 7
                second_parts(b, 0, base)
                low(b, 2)
                early_values(b, 1)
                if not last:
                    dve.wait_ge(x_in, 16 * (NB - 1))
                    variances(x_rows(b + 1), base + 2)
                    second_parts(b, 1, base + 4)
                    low(b + 1, 0)
                    normalise(x_rows(b + 1), zA, z_ok, b + 2, base + 6)
                    second_parts(b, 2, base + 11)
                    low(b + 1, 1)
                else:
                    second_parts(b, 1, base + 2)
                    second_parts(b, 2, base + 4)

            with dve.Fori(0, NB - 2) as b:
                phase_a(b, False)
            phase_a(NB - 2, False)
            phase_a(NB - 1, True)
            A0 = (NB - 1) * A_LINKS + 7 + 6
            dve.wait_ge(consts, 16 * 5)
            chain(V.tensor_copy(gwH[:], gw_raw[:]), A0 + 1)
            V.tensor_tensor(gwL[:], gw_raw[:], gwH[:].bitcast(F32), ALU.subtract).then_inc(gw_ok, 1)

            B0 = A0 + 1

            def reduce_tile(t, parity, i):
                dve.wait_ge(m_full, t + 1)
                V.tensor_reduce(mneg[:, parity, i:i + 1], psM[:, i % 2], X_AXIS, ALU.max,
                                negate=True).then_inc(m_free, 1)

            for i in range(FIRST):
                reduce_tile(TILES + i, 1, i)
            B1 = B0
            U_LINKS = 1

            def unit(b, u, last):
                n = 4 * b + u
                before_router = 9 if last and u == NG - 1 else 0
                links = B1 + U_LINKS * n + before_router
                for k in range(KT):
                    for j, off, i in max_tiles(u, k):
                        if exists(last, u + off):
                            reduce_tile(AHEAD + TILES * n + j, (u + off) % 2, i)
                    stage = router_stage(u, k, last)
                    if stage == 0:
                        dve.wait_ge(c_in, 16 * 4)
                        dve.wait_ge(tanh_ok, 1)
                        dve.wait_ge(cw_ones, 1)
                    if stage in beside_attention:
                        f, before = beside_attention[stage]
                        f(0, links + before - before_router)
                dve.wait_ge(ot_full, n + 1)
                dve.wait_ge(o_taken, n + 1)
                o = psO[:, u % 2].rearrange("p (h v) -> p h v", v=VW)
                used = U_LINKS + ({NG - 2: 9, NG - 1: RL - 9}.get(u, 0) if last else 0)
                chain(V.reciprocal(rden[:], o[:, :, DH]), links + used)
                dve.wait_ge(a_st[u % 2], 16 * (2 * b + u // 2 + 1))
                V.tensor_tensor(ast[:, u % 2].rearrange("p t (h d) -> p (t h) d", d=DH), o[:, :, 0:DH],
                                rden[:].unsqueeze(2).to_broadcast([P, QT * HG, DH]), ALU.mult).then_inc(o_taken, 1)

            def r_residual(b, base):
                if not isinstance(b, int):
                    dve.wait_ge(out_st, 16 * b)
                dve.wait_ge(wo_full, b + 1)
                V.tensor_tensor(z2[:], psX[:].rearrange("p a (t d) -> p (a t) d", d=D),
                                bo_s[:].unsqueeze(1).to_broadcast([P, QT, D]), ALU.add).then_inc(dchain, 1)
                dve.wait_ge(dchain, base + 1)
                rows = xs[:, bass.ds(b * QT, QT)]
                chain(V.scalar_tensor_tensor(out=rows, in0=z2[:], scalar=tg[:, 0:1], in1=rows, op0=ALU.mult,
                                             op1=ALU.add), base + 2)
                variances(x_rows(b), base + 2)

            def r_norm(b, base):
                normalise(x_rows(b), z2, z2_ok, NB + 1 + b, base)

            def r_low(b, base):
                for k in range(DT):
                    dve.wait_ge(zt_hi, 2 * b + k + 1)
                    V.tensor_tensor(zTL[:, bass.ds(b % 2, 1), k].rearrange("p a c -> p (a c)"), psX[:, k],
                                    zTH[:, bass.ds(b % 2, 1), k].bitcast(F32).rearrange("p a c -> p (a c)"),
                                    ALU.subtract).then_inc(zt_ok, 1)

            def r_shift(b, base):
                dve.wait_ge(lt_full, b + 1)
                lg = psX[:, 1, 0:QT * NR].rearrange("p (t e) -> p t e", e=NR)
                chain(V.tensor_reduce(small[:, 0], lg, X_AXIS, ALU.max, negate=True), base + 1)
                V.tensor_tensor(pt[:, 0], lg, small[:, 0].unsqueeze(2).to_broadcast([P, QT, NR]),
                                ALU.add).then_inc(d_ok, 1)

            def r_choose(b, base):
                dve.wait_ge(ex_ok, b + 1)
                chain(V.tensor_reduce(small[:, 1], pt[:, 1], X_AXIS, ALU.add), base + 1)
                chain(V.reciprocal(small[:, 2], small[:, 1]), base + 2)
                chain(V.tensor_tensor(pt[:, 2], pt[:, 1], small[:, 2].unsqueeze(2).to_broadcast([P, QT, NR]),
                                      ALU.mult), base + 3)
                for t in range(QT):
                    rows = slice(t * NR, (t + 1) * NR)
                    other = pt[:, 2, t].unsqueeze(1).to_broadcast([P, NR, NR])
                    own = pt[:, 2, t].unsqueeze(2).to_broadcast([P, NR, NR])
                    V.tensor_tensor(cmp[:, 0, rows], other, own, ALU.is_gt)
                    last = V.tensor_tensor(cmp[:, 1, rows], other, own, ALU.is_equal)
                chain(last, base + 4)
                for t in range(QT):
                    rows = slice(t * NR, (t + 1) * NR)
                    last = V.tensor_tensor(cmp[:, 1, rows], cmp[:, 1, rows], trimask[:], ALU.mult)
                chain(last, base + 5)
                chain(V.tensor_tensor(cmp[:, 0], cmp[:, 0], cmp[:, 1], ALU.add), base + 6)
                chain(V.tensor_reduce(rank[:], cmp[:, 0], X_AXIS, ALU.add), base + 7)
                V.scalar_tensor_tensor(out=pt[:, 3].rearrange("p t e -> p (t e)"), in0=rank[:], scalar=1.5,
                                       in1=pt[:, 2].rearrange("p t e -> p (t e)"), op0=ALU.is_lt,
                                       op1=ALU.mult).then_inc(cw_ok, 1)

            router = {1: (r_residual, 0), 2: (r_norm, 4), 3: (r_low, 9), 5: (r_shift, 9), 6: (r_choose, 10)}
            beside_attention = {1: (r_residual, 0), 4: (r_norm, 4), 6: (r_low, 9), 8: (r_shift, 9), 9: (r_choose, 10)}
            RL = 17

            with dve.Fori(0, NB - 1) as b:
                for u in range(NG):
                    unit(b, u, False)
            for u in range(NG):
                unit(NB - 1, u, True)
            C1 = B1 + U_LINKS * (UNITS - 1) + RL + 1
            E_LINKS = 2 * NR + RL

            def gate(b, e, j, value):
                dve.wait_ge(sil_ok, 18 * b + 2 * e + j + 1)
                if e:
                    if j == 0:
                        dve.wait_ge(cwb_ld[e % 2], 16 * (4 * b + (e + 1) // 2))
                    chain(V.tensor_tensor(sil[:, j], sil[:, j], cwb[:, e % 2], ALU.mult), value)
                elif not isinstance(b, int):
                    dve.wait_ge(gl_ok, 18 * b - 1 + j)
                V.scalar_tensor_tensor(out=g[:, j], in0=psH[:, j, 1], scalar=b1_s[:, e, 2 + j:3 + j],
                                       in1=sil[:, j], op0=ALU.add, op1=ALU.mult).then_inc(g_ok, 1)

            def gated_low(b, e, j):
                dve.wait_ge(gh_ok, 18 * b + 2 * e + j + 1)
                V.tensor_tensor(gL[:, e % 2, j], g[:, j], gH[:, e % 2, j].bitcast(F32),
                                ALU.subtract).then_inc(gl_ok, 1)

            for s in range(2):
                dve.wait_ge(a_st[s], 16 + 16 * UNITS // 2)
            gate(0, 0, 0, 0)
            gate(0, 0, 1, 0)
            gated_low(0, 0, 0)

            def experts(b, last):
                links = C1 + E_LINKS * b
                count = 0
                for e in range(1, NE):
                    count += 1
                    gate(b, e, 0, links + count)
                    gated_low(b, e - 1, 1)
                    count += 1
                    gate(b, e, 1, links + count)
                    gated_low(b, e, 0)
                    if not last and e - 1 in router:
                        f, before = router[e - 1]
                        f(b + 1, links + count)
                        count += {1: 4, 2: 5, 3: 0, 5: 1, 6: 7}[e - 1]
                gated_low(b, NE - 1, 1)
                if not last:
                    gate(b + 1, 0, 0, 0)
                    gate(b + 1, 0, 1, 0)
                    gated_low(b + 1, 0, 0)
                dve.wait_ge(yt_full, b + 1)
                if last:
                    dve.wait_ge(out_st, 16 * (b + 1))
                V.scalar_tensor_tensor(out=o_s[:], in0=psY[:].rearrange("p a (t d) -> p (a t) d", d=D),
                                       scalar=tg[:, 1:2], in1=xs[:, bass.ds(b * QT, QT)], op0=ALU.mult,
                                       op1=ALU.add).then_inc(y_taken, 1)

            with dve.Fori(0, NB - 1) as b:
                experts(b, False)
            experts(NB - 1, True)

        @block.tensor
        def _(pe):
            mm, tr = nc.tensor.matmul, nc.tensor.transpose

            pe.wait_ge(idn_in, 16)

            def turn(b):
                pe.wait_ge(z_ok, b + 1)
                for k in range(DT):
                    for t in range(QT):
                        last = tr(psT[:, k, t * P:(t + 1) * P], zA[:, t, k * P:(k + 1) * P], idn[:])
                    last.then_inc(t_full, 1)

            def turn_max(n, parity, tiles, first=False):
                pe.wait_ge(m_free, 2 + tiles)
                if not first:
                    pe.wait_ge(o_taken, n)
                tr(psO[0:TILES, parity, 0:P], mneg[:, parity], idn[:]).then_inc(mt_full, 1)

            def early(b, c, place):
                for i in early_tiles(b, c, place):
                    if i == 0:
                        pe.wait_ge(unit_ld[0], 16 * 12)
                    else:
                        pe.wait_ge(m_free, 2 + i)
                    h, qt = divmod(i, QT)
                    for half in range(2):
                        last = mm(psE[:, half * BLK:(half + 1) * BLK],
                                  qst[0:SROWS, 0, h, qt * P:(qt + 1) * P],
                                  kst[0:SROWS, 0, h, half * BLK:(half + 1) * BLK], start=True, stop=True)
                    last.then_inc(m_full, 1)

            def project(b, c):
                pe.wait_ge(t_split, 6 * b + 2 * c + 2)
                terms = ((wAH, tH), (wAL, tH), (wAH, tL))
                if c < 2:
                    for t in range(QT):
                        if t % 2 == 0:
                            pe.wait_ge(v_taken, 4 * b + 2 * c + t // 2 + 1)
                        for i, (wt, tt) in enumerate(terms):
                            for k in range(DT):
                                last = mm(psV[:, t // 2, t % 2], tt[:, c, k, t * P:(t + 1) * P], wt[:, 2, k],
                                          start=(i == 0 and k == 0), stop=(i == 2 and k == DT - 1))
                        if t % 2:
                            last.then_inc(v_full, 1)
                        early(b, c, f"v{t}")
                w = 0 if c == 2 else 1
                if c == 2:
                    pe.wait_ge(wA_ok, 2)
                for m in range(DT):
                    pe.wait_ge(f_taken, 6 * b + 2 * c + m + 1)
                    for i, (wt, tt) in enumerate(terms):
                        for k in range(DT):
                            last = mm(psF[:, m], wt[:, w, k, m * P:(m + 1) * P], tt[:, c, k],
                                      start=(i == 0 and k == 0), stop=(i == 2 and k == DT - 1))
                    last.then_inc(f_full, 1)
                    early(b, c, f"f{m}")
                    if m == 0 and c == 2 and isinstance(b, int) and b == NB - 1:
                        turn_max(0, 0, TILES, first=True)

            def phase_a(b, last):
                project(b, 0)
                turn(b)
                project(b, 1)
                project(b, 2)

            pe.wait_ge(wA_ok, 1)
            with pe.Fori(0, NB - 2) as b:
                phase_a(b, False)
            phase_a(NB - 2, False)
            phase_a(NB - 1, True)

            def max_tile(t, slot, i):
                h, qt = divmod(i, QT)
                pe.wait_ge(m_free, t + 1)
                for half in range(2):
                    last = mm(psM[:, i % 2, half * BLK:(half + 1) * BLK],
                              qst[0:SROWS, slot, h, qt * P:(qt + 1) * P],
                              kst[0:SROWS, slot, h, half * BLK:(half + 1) * BLK], start=True, stop=True)
                last.then_inc(m_full, 1)

            def score_tile(s, slot, kt, j):
                if isinstance(s, int) and s >= TAIL:
                    if s == TAIL and j >= 2:
                        pe.wait_ge(m_free, 2 + UNITS * TILES)
                    elif s == TAIL:
                        pe.wait_ge(e_done, 4 * s + j + 1)
                    else:
                        pe.wait_ge(e_done, 2 + 4 * (s - 1) + j + 1)
                else:
                    pe.wait_ge(e_done, 4 * s + j + 1)
                mm(score_bank(s, j), kst[:, slot, j, kt * P:(kt + 1) * P], qst[:, slot, j], start=True,
                   stop=True).then_inc(s_full, 1)

            pe.wait_ge(f_taken, 2 + 6 * NB)
            pe.wait_ge(v_taken, 2 + 4 * NB)
            pe.wait_ge(ones_k, 1)
            pe.wait_ge(unit_ld[1], 16 * 12)
            BEFORE = 5
            for i in range(FIRST):
                max_tile(TILES + i, 1, i)
                if i == BEFORE:
                    pe.wait_ge(m_ld[0], 48)
                if i >= BEFORE:
                    score_tile((i - BEFORE) // HG, 0, (i - BEFORE) // HG, (i - BEFORE) % HG)
            for i in range(FIRST - BEFORE, LEAD * HG):
                score_tile(i // HG, 0, i // HG, i % HG)

            def values(b, u, k):
                n = 4 * b + u
                if k == 0:
                    pe.wait_ge(mt_copied, n + 1)
                    pe.wait_ge(v_ld[u], 16 * (b + 1))
                pe.wait_ge(e_done, 2 + 4 * (8 * n + k + 1))
                for j in range(HG):
                    last = mm(psO[j * VW:(j + 1) * VW, u % 2], vt[:, u, k, j * VW:(j + 1) * VW], pr[:, k % 4, j],
                              start=(k == 0), stop=(k == KT - 1), skip_group_check=True)
                last.then_inc(pv_done, 1)

            def unit(b, u, last):
                n = 4 * b + u
                for k in range(KT):
                    nxt, kt = divmod(k + LEAD, KT)
                    slot = (u + nxt) % NG
                    ahead = exists(last, u + nxt)
                    tiles = [(j, off, i) for j, off, i in max_tiles(u, k) if exists(last, u + off)]
                    if ahead and kt == 0:
                        pe.wait_ge(m_ld[slot], 48 * (b + 1 + (u + 1) // NG))

                    def score(j):
                        if ahead:
                            score_tile(8 * n + k + LEAD, slot, kt, j)

                    score(0)
                    score(1)
                    values(b, u, k)
                    score(2)
                    score(3)
                    for j, off, i in tiles:
                        if off == 2 and i == 0:
                            pe.wait_ge(unit_ld[(u + 2) % NG], 16 * 12 * (b + 1 + (u + 2) // NG))
                        max_tile(AHEAD + TILES * n + j, (u + off) % NG, i)
                    if k == MAX_TURN and exists(last, u + 1):
                        turn_max(n + 1, (u + 1) % 2, AHEAD + TILES * n + REST)
                    stage = router_stage(u, k, last)
                    if stage == 0:
                        pe.wait_ge(c_in, 16 * 4)
                        pe.wait_ge(gw_ok, 1)
                        pe.wait_ge(m_free, 2 + UNITS * TILES)
                    if stage in beside_attention:
                        beside_attention[stage](0)
                pe.wait_ge(o_copied, n + 1)
                for t in range(QT):
                    fin = tr(psO[:, u % 2, t * P:(t + 1) * P], osb[:, t * P:(t + 1) * P], idn[:])
                fin.then_inc(ot_full, 1)

            def r_attn(b):
                pe.wait_ge(a_ld, 16 * (b + 1))
                if not isinstance(b, int):
                    pe.wait_ge(cwt_ok, b)
                for k in range(DT):
                    for t in range(QT):
                        last = tr(psX[:, k, t * P:(t + 1) * P], a_in[:, t, k * P:(k + 1) * P], idn[:])
                last.then_inc(at_full, 1)

            def r_wo(b):
                pe.wait_ge(at_ok, 2 * b + 2)
                for t in range(QT):
                    for k in range(DT):
                        last = mm(psX[:, t // 2, (t % 2) * D:(t % 2 + 1) * D], aT[:, k, t * P:(t + 1) * P], wo_s[:, k],
                                  start=(k == 0), stop=(k == DT - 1))
                last.then_inc(wo_full, 1)

            def r_turn(b):
                pe.wait_ge(z2_ok, b + 1)
                for k in range(DT):
                    for t in range(QT):
                        last = tr(psX[:, k, t * P:(t + 1) * P], z2[:, t, k * P:(k + 1) * P], idn[:])
                last.then_inc(zt_full, 1)

            def zt(part, b, k):
                return (zTH, zTL)[part][:, bass.ds(b % 2, 1), k].rearrange("p a c -> p (a c)")

            def r_logits(b):
                pe.wait_ge(zt_ok, 2 * b + 2)
                for i, (wt, part) in enumerate(((gwH, 0), (gwL, 0), (gwH, 1))):
                    for k in range(DT):
                        last = mm(psX[0:NR, 0], wt[:, k], zt(part, b, k), start=(i == 0 and k == 0),
                                  stop=(i == 2 and k == DT - 1))
                last.then_inc(lg_full, 1)

            def r_lturn(b):
                pe.wait_ge(lg_sb, b + 1)
                for t in range(QT):
                    last = mm(psX[:, 1, t * NR:(t + 1) * NR], lT[:, t * P:(t + 1) * P], idn[0:NR, 0:NR],
                              start=True, stop=True)
                last.then_inc(lt_full, 1)

            def r_cturn(b):
                pe.wait_ge(cw_ok, b + 1)
                for t in range(QT):
                    last = tr(psX[0:NR, 0, t * P:(t + 1) * P], pt[:, 3, t], idn[:])
                last.then_inc(cwt_full, 1)

            router = {0: r_attn, 1: r_wo, 3: r_turn, 4: r_logits, 5: r_lturn, 7: r_cturn}
            beside_attention = {0: r_attn, 1: r_wo, 6: r_turn, 7: r_logits, 8: r_lturn, 12: r_cturn}

            with pe.Fori(0, NB - 1) as b:
                for u in range(NG):
                    unit(b, u, False)
            for u in range(NG):
                unit(NB - 1, u, True)

            def second(b, e, k, stop=False):
                pe.wait_ge(gl_ok, 18 * b + 2 * e + k + 1)
                if e == 0 and k == 0:
                    pe.wait_ge(y_taken, b + 1)
                for m in range(DT):
                    for i, (part, gt) in enumerate(((0, gH), (1, gH), (0, gL))):
                        last = mm(psY[:, m], w2(e, part)[:, k, m * P:(m + 1) * P], gt[:, e % 2, k],
                                  start=(e == 0 and k == 0 and i == 0), stop=(stop and i == 2))
                if k:
                    last.then_inc(w2_done, 1)

            def first(b, e, j):
                pe.wait_ge(g_ok, 18 * b + 2 * e + j + 1)
                for ab in range(2):
                    m = 2 * ab + j
                    for i, (wp, zp) in enumerate(((0, 0), (1, 0), (0, 1))):
                        for k in range(DT):
                            last = mm(psH[:, j, ab], w1(e, wp)[:, k, m * P:(m + 1) * P], zt(zp, b, k),
                                      start=(i == 0 and k == 0), stop=(i == 2 and k == DT - 1))
                last.then_inc(h_full, 1)

            def turn_sum(b):
                pe.wait_ge(y_copied, 2 * b + 2)
                for t in range(QT):
                    for m in range(DT):
                        last = tr(psY[:, t // 2, (t % 2) * D + m * P:(t % 2) * D + (m + 1) * P],
                                  yT[:, m, t * P:(t + 1) * P], idn[:])
                last.then_inc(yt_full, 1)

            def experts(b, last):
                for e in range(1, NE):
                    pe.wait_ge(w_ok, e + 1)
                    first(b, e, 0)
                    first(b, e, 1)
                    second(b, e - 1, 0)
                    second(b, e - 1, 1)
                    if not last and e - 1 in router:
                        router[e - 1](b + 1)
                if not last:
                    pe.wait_ge(zt_ok, 2 * b + 4)
                    first(b + 1, 0, 0)
                pe.wait_ge(cwt_ok, b + 1)
                for m in range(DT):
                    mm(psY[:, m], b2_s[:, m * P:(m + 1) * P], cw_of(b), start=False, stop=False)
                second(b, NE - 1, 0)
                second(b, NE - 1, 1, stop=True)
                if not last:
                    first(b + 1, 0, 1)
                turn_sum(b)

            pe.wait_ge(w_ok, 1)
            pe.wait_ge(zt_ok, 2)
            first(0, 0, 0)
            first(0, 0, 1)
            pe.wait_ge(o_taken, UNITS + 1)
            with pe.Fori(0, NB - 1) as b:
                experts(b, False)
            experts(NB - 1, True)


def kernel(x, ctx_1024, g_xattn, g_ffn, L0_xattn_Wq, L0_xattn_bq, L0_xattn_Wk, L0_xattn_bk, L0_xattn_Wv,
           L0_xattn_bv, L0_xattn_Wo, L0_xattn_bo, L0_ffn_gate_w, L0_ffn_gate_b, L0_ffn_sw1, L0_ffn_sb1,
           L0_ffn_sw2, L0_ffn_sb2, L0_ffn_rw1, L0_ffn_rb1, L0_ffn_rw2, L0_ffn_rb2):
    import numpy as np
    import concourse.bacc as bacc
    from concourse.bass_utils import run_bass_kernel_spmd

    def rows(w):
        w = np.asarray(w)
        return w.reshape(w.shape[0] // P, P, w.shape[1]).transpose(1, 0, 2)

    def spread(v, n=P):
        return np.broadcast_to(np.asarray(v), (n, np.asarray(v).shape[0]))

    w1 = np.concatenate([np.asarray(L0_ffn_sw1), np.asarray(L0_ffn_rw1)])
    w2 = np.concatenate([np.asarray(L0_ffn_sw2), np.asarray(L0_ffn_rw2)])
    b1 = np.concatenate([np.asarray(L0_ffn_sb1), np.asarray(L0_ffn_rb1)])
    arrays = {
        "x": x, "ctx": np.asarray(ctx_1024).transpose(0, 2, 1),
        "gates": spread(np.concatenate([np.asarray(g_xattn), np.asarray(g_ffn)])),
        "wqkv": np.stack([rows(np.asarray(w).T) for w in (L0_xattn_Wq, L0_xattn_Wk, L0_xattn_Wv)], axis=1),
        "bqkv": np.stack([np.asarray(v).reshape(DT, P).T for v in (L0_xattn_bq, L0_xattn_bk, L0_xattn_bv)], axis=1),
        "wo": rows(np.asarray(L0_xattn_Wo).T), "bo": spread(L0_xattn_bo),
        "gate_w": rows(L0_ffn_gate_w), "gate_b": np.asarray(L0_ffn_gate_b).reshape(NR, 1),
        "wexp": np.stack([np.concatenate([rows(a).reshape(P, -1), rows(c).reshape(P, -1)], axis=1)
                          for a, c in zip(w1, w2)]),
        "b1": b1.reshape(NE, 4, P).transpose(2, 0, 1),
        "b2": np.concatenate([np.asarray(L0_ffn_rb2), np.asarray(L0_ffn_sb2)]),
        "ident": np.eye(P, dtype=np.float32),
        "tri": np.broadcast_to(np.tril(np.ones((NR, NR), np.float32), -1), (P, NR, NR)),
    }
    arrays = {k: np.ascontiguousarray(v) for k, v in arrays.items()}
    nc = bacc.Bacc("TRN2", target_bir_lowering=False, num_devices=1)
    args = [nc.dram_tensor(k, v.shape, mybir.dt.from_np(v.dtype), kind="ExternalInput").ap()
            for k, v in arrays.items()]
    out = nc.dram_tensor("out", (NB, NQ, D), F32, kind="ExternalOutput").ap()
    build(nc, *args, out)
    r = run_bass_kernel_spmd(nc, [arrays], core_ids=[0])
    return r.results[0]["out"]
```
